# Optimizing a Trainium2 kernel written in Bass

```python
import numpy as np
import jax
import jax.numpy as jnp

def _softmax(x, axis=-1):
    return jax.nn.softmax(x, axis=axis)

def _gelu(x):
    return jax.nn.gelu(x, approximate=True)

def _silu(x):
    return jax.nn.silu(x)

def _sigmoid(x):
    return jax.nn.sigmoid(x)

def _layernorm(x, axis=-1, eps=1e-05):
    m = jnp.mean(x, axis=axis, keepdims=True)
    v = jnp.var(x, axis=axis, keepdims=True)
    return (x - m) / jnp.sqrt(v + eps)

def _scatter_add(tgt, idx, src, axis=0):
    return tgt.at[idx].add(src)

def _segment_sum(src, seg, n):
    return jax.ops.segment_sum(src, seg, n)
kernel_name = 'mk_macaron_d1_jaxref_r8_38d75e'

def setup_inputs(seed: int=0):
    np.random.seed(seed)
    _w = jnp.asarray

    def _L0_attn_setup():
        import jax, jax.numpy as jnp
        import numpy as np
        D_MODEL = 128
        Q_HEADS = 16
        KV_HEADS = 4
        HEAD_DIM = D_MODEL // Q_HEADS
        KV_DIM = HEAD_DIM * KV_HEADS
        GROUPS = Q_HEADS // KV_HEADS
        LN_EPS = 1e-05
        NEG_INF = -10000000000.0
        key = jax.random.key(seed)
        ks = jax.random.split(key, 6)
        b, n = (2, 256)

        def xavier(k, fan_in, fan_out):
            limit = np.sqrt(6.0 / (fan_in + fan_out)).astype(np.float32)
            return jax.random.uniform(k, (fan_in, fan_out), jnp.float32, -limit, limit)
        return {'x': jax.random.normal(ks[0], (b, n, D_MODEL), jnp.float32), 'Wq': xavier(ks[1], D_MODEL, D_MODEL), 'bq': jnp.zeros((D_MODEL,), jnp.float32), 'Wk': xavier(ks[2], D_MODEL, KV_DIM), 'bk': jnp.zeros((KV_DIM,), jnp.float32), 'Wv': xavier(ks[3], D_MODEL, KV_DIM), 'bv': jnp.zeros((KV_DIM,), jnp.float32), 'ln_g': jnp.ones((D_MODEL,), jnp.float32), 'ln_b': jnp.zeros((D_MODEL,), jnp.float32), 'Wo': xavier(ks[4], D_MODEL, D_MODEL), 'bo': jnp.zeros((D_MODEL,), jnp.float32)}
    _L0_attn_in = _L0_attn_setup()

    def _L0_ffn_setup():
        import jax, jax.numpy as jnp
        import numpy as np
        DIM = 128
        HIDDEN = 384
        SCALE = 1.0 / 127.0

        def _dequant(w_int, dtype):
            return w_int.astype(dtype) * jnp.asarray(SCALE, dtype)
        key = jax.random.key(seed)
        k_x, k_g, k_u, k_d = jax.random.split(key, 4)
        x = jax.random.normal(k_x, (4, 256, DIM), dtype=jnp.float32)
        w_gate = jax.random.randint(k_g, (HIDDEN, DIM), -127, 128, dtype=jnp.int32)
        w_up = jax.random.randint(k_u, (HIDDEN, DIM), -127, 128, dtype=jnp.int32)
        w_down = jax.random.randint(k_d, (DIM, HIDDEN), -127, 128, dtype=jnp.int32)
        return {'x': x, 'w_gate': w_gate, 'w_up': w_up, 'w_down': w_down}
    _L0_ffn_in = _L0_ffn_setup()
    _d = {'L0_attn_x': _L0_attn_in['x'], 'L0_attn_Wq': _L0_attn_in['Wq'], 'L0_attn_bq': _L0_attn_in['bq'], 'L0_attn_Wk': _L0_attn_in['Wk'], 'L0_attn_bk': _L0_attn_in['bk'], 'L0_attn_Wv': _L0_attn_in['Wv'], 'L0_attn_bv': _L0_attn_in['bv'], 'L0_attn_ln_g': _L0_attn_in['ln_g'], 'L0_attn_ln_b': _L0_attn_in['ln_b'], 'L0_attn_Wo': _L0_attn_in['Wo'], 'L0_attn_bo': _L0_attn_in['bo'], 'L0_ffn_w_gate': _L0_ffn_in['w_gate'], 'L0_ffn_w_up': _L0_ffn_in['w_up'], 'L0_ffn_w_down': _L0_ffn_in['w_down']}
    _x0 = _d['L0_attn_x']
    _d['L0_attn_x'] = jax.random.normal(jax.random.fold_in(jax.random.key(seed), 1), (8, 512, 128), dtype=_x0.dtype)
    del _x0
    return _d

def reference(L0_attn_x, L0_attn_Wq, L0_attn_bq, L0_attn_Wk, L0_attn_bk, L0_attn_Wv, L0_attn_bv, L0_attn_ln_g, L0_attn_ln_b, L0_attn_Wo, L0_attn_bo, L0_ffn_w_gate, L0_ffn_w_up, L0_ffn_w_down):

    def _L0_attn_ref(x, Wq, bq, Wk, bk, Wv, bv, ln_g, ln_b, Wo, bo):
        import jax, jax.numpy as jnp
        import numpy as np
        D_MODEL = 128
        Q_HEADS = 16
        KV_HEADS = 4
        HEAD_DIM = D_MODEL // Q_HEADS
        KV_DIM = HEAD_DIM * KV_HEADS
        GROUPS = Q_HEADS // KV_HEADS
        LN_EPS = 1e-05
        NEG_INF = -10000000000.0
        b, n, _ = x.shape
        q = x @ Wq + bq
        k = x @ Wk + bk
        v = x @ Wv + bv
        q = q.reshape(b, n, GROUPS, KV_HEADS, HEAD_DIM)
        q = jnp.transpose(q, (0, 2, 3, 1, 4))
        k = k.reshape(b, n, KV_HEADS, HEAD_DIM)
        v = v.reshape(b, n, KV_HEADS, HEAD_DIM)
        scale = jnp.asarray(HEAD_DIM ** 0.5, q.dtype)
        q = q / scale
        attn_logits = jnp.einsum('bghnd,bmhd->bghnm', q, k)
        causal = jnp.tril(jnp.ones((n, n), dtype=bool))
        attn_logits = jnp.where(causal[None, None, None, :, :], attn_logits, NEG_INF)
        attn = jax.nn.softmax(attn_logits, axis=-1)
        out = jnp.einsum('bghnm,bmhd->bghnd', attn, v)
        out = jnp.transpose(out, (0, 3, 1, 2, 4)).reshape(b, n, D_MODEL)
        mu = jnp.mean(out, axis=-1, keepdims=True)
        var = jnp.var(out, axis=-1, keepdims=True)
        out = (out - mu) * jax.lax.rsqrt(var + LN_EPS) * ln_g + ln_b
        out = out @ Wo + bo
        return out

    def _L0_ffn_ref(x, w_gate, w_up, w_down):
        import jax, jax.numpy as jnp
        import numpy as np
        DIM = 128
        HIDDEN = 384
        SCALE = 1.0 / 127.0

        def _dequant(w_int, dtype):
            return w_int.astype(dtype) * jnp.asarray(SCALE, dtype)
        wg = _dequant(w_gate, x.dtype)
        wu = _dequant(w_up, x.dtype)
        wd = _dequant(w_down, x.dtype)
        gate = jnp.einsum('bsd,hd->bsh', x, wg)
        up = jnp.einsum('bsd,hd->bsh', x, wu)
        h = jax.nn.silu(gate) * up
        return jnp.einsum('bsh,dh->bsd', h, wd)
    x = L0_attn_x
    x = x + 0.5 * _L0_ffn_ref(_layernorm(x, axis=-1), L0_ffn_w_gate, L0_ffn_w_up, L0_ffn_w_down)
    x = x + _L0_attn_ref(_layernorm(x, axis=-1), L0_attn_Wq, L0_attn_bq, L0_attn_Wk, L0_attn_bk, L0_attn_Wv, L0_attn_bv, L0_attn_ln_g, L0_attn_ln_b, L0_attn_Wo, L0_attn_bo)
    x = x + 0.5 * _L0_ffn_ref(_layernorm(x, axis=-1), L0_ffn_w_gate, L0_ffn_w_up, L0_ffn_w_down)
    return x

_drawn_inputs = setup_inputs


def setup_inputs(seed=0):
    import zlib

    import numpy as np

    out = dict(_drawn_inputs(seed))
    spreads = {'L0_attn_bq': (0.0, 0.8),
     'L0_attn_bk': (0.0, 0.8),
     'L0_attn_bv': (0.0, 0.8),
     'L0_attn_ln_g': (1.0, 0.6),
     'L0_attn_ln_b': (0.0, 0.8),
     'L0_attn_bo': (0.0, 0.8)}
    factors = {'L0_attn_Wq': 8.0, 'L0_attn_Wk': 8.0, 'L0_attn_Wv': 8.0, 'L0_attn_Wo': 7.215}
    for name, (base, spread) in spreads.items():
        noise = np.random.default_rng([zlib.crc32(name.encode()), seed]).standard_normal(out[name].shape)
        drawn = base * np.exp(spread * noise) if base else spread * noise
        out[name] = jnp.asarray(drawn.astype(out[name].dtype))
    for name, factor in factors.items():
        out[name] = (out[name] * factor).astype(out[name].dtype)
    return out
```

```python
from contextlib import ExitStack

import numpy as np

import concourse.bass as bass
from concourse import mybir

F32 = mybir.dt.float32
F16 = mybir.dt.float16
BF16 = mybir.dt.bfloat16
I32 = mybir.dt.int32
ALU = mybir.AluOpType
ACT = mybir.ActivationFunctionType
AX = mybir.AxisListType

P = 128
ENTRIES, TOKENS, D = 8, 512, 128
TILES = TOKENS // P
G, H, HD = 4, 4, 8
KB = 32
BLOCKS = TOKENS // KB
CHUNKS = 3
HIDDEN = CHUNKS * P
EPS = 1e-5
WSCALE = 2.0 ** -7
QSCALE = float(HD) ** -0.5
TANH_SCALE = 0.5 * 128.0 / 127.0
FFN_SCALE = 0.25 * (128.0 / 127.0) ** 3
MASKED = -1e30
PROBS_RING = 8
ADDED = 9

PACK = {}
_at = 0
for _name, _n in (("wqkv", G * P + 2 * P), ("wo", D), ("ln_b", P), ("bo", D),
                  ("bq", G), ("bk", 1), ("bv", 1), ("ln_g", 1), ("ident", P), ("mask_s", P), ("mask_t", P),
                  ("eye", KB), ("block", H * HD), ("low_q", 1), ("low_k", 1), ("neg_half", TILES), ("eps", TILES), ("zero", 1)):
    PACK[_name] = (_at, _at + _n)
    _at += _n
PACKED = _at


def timeline():
    items = [("A", "keys", 0)] + [("A", "queries", g) for g in range(G)]
    items += [("B", "sums", 0), ("A", "values", 0)]
    back = [("turn_out", 0), ("stats", "inner"), ("norm", "inner"), ("turn", "inner"), ("out_proj", 0),
            ("stats", "ln3"), ("norm", "ln3"), ("turn", "ln3"),
            ("hidden", 0), ("hidden", 1), ("hidden", 2), ("down", 0)]
    at = dict(zip((3, 5, 7, 9, 12, 14, 17, 19, 22, 25, 28, 32), back))
    for s, (t, heads) in enumerate(SCORE_TILES):
        items.append(("A", "scores", s))
        if s in at:
            items.append(("B",) + at[s])
        if s == 20:
            items.append(("A", "carry", 0))
        if s + 1 == FIRST_HALF:
            items.append(("A", "maxima", 0))
    items.append(("A", "maxima", 1))
    front = [("stats", "ln1"), ("norm", "ln1"), ("turn", "ln1"), ("hidden", 0), ("hidden", 1),
             ("hidden", 2), ("down", 0), ("stats", "ln2"), ("norm", "ln2"), ("turn", "ln2")]
    at = dict(zip((-1, 0, 1, 2, 3, 4, 6, 8, 9, 11), front))
    items.append(("F",) + at[-1])
    for u in range(BLOCKS):
        items.append(("A", "probs", u))
        if u:
            items.append(("A", "mix", u - 1))
        if u in at:
            items.append(("F",) + at[u])
    items.append(("A", "mix", BLOCKS - 1))
    return items


SCORE_TILES = [(t, tuple(range(h, h + n))) for t in range(BLOCKS)
               for n in ((4 if t < 4 else 2 if t < 8 else 1),) for h in range(0, H, n)]
FIRST_HALF = sum(t < BLOCKS // 2 for t, _ in SCORE_TILES)

def work_uses(item):
    stage, what, k = item
    n = {"keys": 1, "queries": 1, "values": 1, "scores": 1, "sums": 1, "turn_out": 2, "turn": 1,
         "hidden": 2, "down": 1, "out_proj": 1}.get(what, 0)
    return [(stage, what, k, j) for j in range(n)]


WORK = 3
TIMELINE = timeline()
USES = [u for item in TIMELINE for u in work_uses(item)]
SLOT = {u: i % WORK for i, u in enumerate(USES)}
PER = {s: {stage: sum(1 for u in USES if SLOT[u] == s and u[0] == stage) for stage in "FAB"}
       for s in range(WORK)}

UNITS = [(u, gs, n) for u in range(BLOCKS)
         for gs, n in ([((0, 1), 1), ((2, 3), 1)] if TOKENS - KB * u > 256 else [((0, 1, 2, 3), 2)])]
UNITS_UPTO = [sum(1 for v, _, _ in UNITS if v <= u) for u in range(BLOCKS)]


class Step:

    def __init__(self, b, stages):
        self.b, self.stages = b, stages
        if isinstance(b, int):
            self.before = {"F": min(b + 1, ENTRIES), "A": max(b, 0), "B": max(b - 1, 0)}
        else:
            self.before = {"F": b + 1, "A": b, "B": b - 1}

    def items(self):
        return [i for i in TIMELINE if i[0] in self.stages]

    def upto(self, stage, per, k):
        return self.before[stage] * per + k

    def work(self, use):
        s = SLOT[use]
        rank = sum(1 for u in USES[:USES.index(use) + 1] if SLOT[u] == s and u[0] in self.stages)
        n = self.before
        return n["F"] * PER[s]["F"] + n["A"] * PER[s]["A"] + (n["B"] * PER[s]["B"] + rank)

    def work_before(self, slot):
        n = self.before
        return n["F"] * PER[slot]["F"] + n["A"] * PER[slot]["A"] + n["B"] * PER[slot]["B"]


def wait_for(eng, sem, value):
    if not isinstance(value, int) or value > 0:
        eng.wait_ge(sem, value)


def macaron(nc, x, packed, wgu, wd, out):
    x_v = x.rearrange("e (i p) d -> e p i d", p=P)
    out_v = out.rearrange("e (i p) d -> e p i d", p=P)
    with ExitStack() as ctx:
        def sb(name, shape, dt=F32):
            return ctx.enter_context(nc.sbuf_tensor(name, [P] + shape, dt))

        def sem(name):
            return ctx.enter_context(nc.semaphore(name))

        params = sb("params", [PACKED])

        def par(name):
            a, z = PACK[name]
            return params[:, a:z]

        wgu_i = sb("wgu_i", [2 * HIDDEN], I32)
        wd_i = sb("wd_i", [HIDDEN], I32)
        wgu_s = sb("wgu_s", [2 * HIDDEN], F16)
        wd_s = sb("wd_s", [HIDDEN], F16)
        NQKV = G * P + 2 * P
        w_hi = sb("w_hi", [NQKV], F16)
        w_lo = sb("w_lo", [NQKV], F16)
        wo_g = sb("wo_g", [D])
        wo_hi = sb("wo_hi", [D], F16)
        wo_lo = sb("wo_lo", [D], F16)
        bo_all = sb("bo_all", [D])
        bq_s = sb("bq_s", [G])
        mask_s = sb("mask_s_b", [P], BF16)
        mask_t = sb("mask_t_b", [P], BF16)
        eye = sb("eye_b", [KB], BF16)
        ident = par("ident")
        WK, WV = G * P, G * P + P

        x_in = sb("x_in", [TILES, D])
        x_front = sb("x_front", [TILES, D])
        x_mid = sb("x_mid", [TILES, D])
        x_att = sb("x_att", [TILES, D])
        y = sb("y", [TILES, D])
        ln = {}
        for name in ("ln1", "ln2", "inner", "ln3"):
            ln[name] = dict(
                bn=sb(f"{name}_bn", [TILES, 6]), mv=sb(f"{name}_mv", [TILES, 2]), rstd=sb(f"{name}_rstd", [TILES]),
                var=sb(f"{name}_var", [TILES]), s_var=sem(f"{name}_var_eps"),
                xn=sb(f"{name}_xn", [TILES, D]), hi=sb(f"{name}_hi", [TOKENS], F16), lo=sb(f"{name}_lo", [TOKENS], F16),
                s_bn=sem(f"{name}_tile_stats"), s_mv=sem(f"{name}_moments"), s_rstd=sem(f"{name}_rstd_ready"),
                s_xn=sem(f"{name}_normalised"), s_hi=sem(f"{name}_high_part"))
        gate = sb("gate", [1])
        attended = sb("attended", [TILES, D])
        ln["ln1"]["src"], ln["ln2"]["src"], ln["inner"]["src"], ln["ln3"]["src"] = x_in, x_front, attended, x_att
        ffn = {}
        for st in "FB":
            ffn[st] = dict(
                th=sb(f"{st}_th", [CHUNKS, TOKENS]), a=sb(f"{st}_a", [CHUNKS, TOKENS]), h=sb(f"{st}_h", [CHUNKS, TOKENS]),
                hi=sb(f"{st}_hhi", [CHUNKS, TOKENS], F16), lo=sb(f"{st}_hlo", [CHUNKS, TOKENS], F16),
                s_th=sem(f"{st}_tanh_ready"), s_hi=sem(f"{st}_hidden_high"), s_lo=sem(f"{st}_hidden_low"))
        q_hi = sb("q_hi", [2, TOKENS], F16)
        q_f = sb("q_f", [2, TOKENS])
        q_rows = sb("q_rows", [BLOCKS, G, KB], F16)
        k_rows = sb("k_rows", [TOKENS], F16)
        k_diag = sb("k_diag", [BLOCKS, H, KB], F16)
        v_turned = sb("v_turned", [TOKENS])
        v_diag = sb("v_diag", [BLOCKS, H * HD])
        m_all = sb("m_all", [2, H, 8])
        m_parts = sb("m_parts", [2, 2, KB], F16)
        m_turned = sb("m_turned", [2, 2, KB], F16)
        probs = sb("probs", [PROBS_RING, G, TOKENS])
        prob_sum = sb("prob_sum", [G, TOKENS])
        num_t = sb("num_t", [TOKENS])
        den_t = sb("den_t", [TOKENS])
        rden = sb("rden", [TILES * G * H])

        work = ctx.enter_context(nc.psum_tensor("work", [P, WORK, 512], F32))
        mix = ctx.enter_context(nc.psum_tensor("mix", [P, 512], F32))
        st_ps = ctx.enter_context(nc.psum_tensor("st_ps", [P, 2, 2, 512], F32))

        def bank(use):
            return work[:, SLOT[use], :]

        params_loaded, ints_loaded, x_loaded, y_free = sem("params_loaded"), sem("ints_loaded"), sem("x_loaded"), sem("y_free")
        weights_ready, wo_scaled, w_high, bias_product = sem("weights_ready"), sem("wo_scaled"), sem("w_high"), sem("bias_product")
        k_cleared = sem("k_diag_cleared")
        filled = [sem(f"work{s}_filled") for s in range(WORK)]
        drained = [sem(f"work{s}_drained") for s in range(WORK)]
        q_high, q_done, k_done, k_placed = sem("q_high"), sem("q_rows_ready"), sem("k_rows_ready"), sem("k_diag_ready")
        v_done = sem("v_diag_ready")
        m_high, m_split, m_turn, m_in_rows = sem("m_high"), sem("m_split"), sem("m_turned_ready"), sem("m_in_q_rows")
        st_filled, exp_done, mix_done, sum_done = sem("st_filled"), sem("exp_done"), sem("mix_done"), sem("prob_sum_done")
        num_out = sem("num_out")
        x_mid_done = sem("x_mid_done")
        SETUP = 9

        block = ctx.enter_context(nc.Block())

        def run(eng, piece):
            for b, stages in ((-1, "F"), (0, "FA")):
                step(eng, piece, Step(b, stages))
            with eng.Fori(1, ENTRIES - 1) as b:
                step(eng, piece, Step(b, "FAB"))
            for b, stages in ((ENTRIES - 1, "AB"), (ENTRIES, "B")):
                step(eng, piece, Step(b, stages))

        def step(eng, piece, st):
            for item in st.items():
                piece(st, *item)

        def wait_drained(eng, st, use):
            eng.wait_ge(drained[SLOT[use]], st.work(use))

        def wait_filled(eng, st, use):
            eng.wait_ge(filled[SLOT[use]], st.work(use))

        @block.sync
        def _(sp):
            sp.dma_start(x_in[:, :, :], x_v[0]).then_inc(x_loaded, 16)
            sp.dma_start(params[:, :], packed).then_inc(params_loaded, 16)
            sp.dma_start(wgu_i[:, :], wgu).then_inc(ints_loaded, 16)
            sp.dma_start(wd_i[:, :], wd).then_inc(ints_loaded, 16)

            def piece(st, stage, what, k):
                if what == "carry" and "F" in st.stages:
                    sp.wait_ge(x_mid_done, st.upto("A", 1, 1))
                    sp.dma_start(x_in[:, :, :], x_v[bass.ds(st.b + 1, 1)].rearrange("a p i d -> p (a i) d")
                                 ).then_inc(x_loaded, 16)
                if what == "maxima":
                    sp.wait_ge(m_turn, st.upto("A", 2, k + 1))
                    for g in range(G):
                        for part in range(2):
                            row = 3 * HD + part
                            sp.dma_start(
                                q_rows[row:row + 3 * KB + 1:KB, 8 * k:8 * k + 8, g, :],
                                m_turned[KB * g:KB * g + KB, k, part, :]).then_inc(m_in_rows, 16)
                if (stage, what) == ("B", "down"):
                    wait_drained(sp, st, (stage, what, k, 0))
                    sp.dma_start(out_v[bass.ds(st.b - 1, 1)].rearrange("a p i d -> p (a i) d"), y[:, :, :]
                                 ).then_inc(y_free, 16)

            run(sp, piece)
            sp.wait_ge(y_free, 16 + 16 * ENTRIES)

        @block.tensor
        def _(pe):
            mm = nc.tensor.matmul
            pe.wait_ge(params_loaded, 16)
            mm(mix[:, 0:D], par("ln_b"), par("wo"), start=True, stop=True).then_inc(bias_product, 1)
            pe.wait_ge(weights_ready, SETUP)
            pe.wait_ge(k_cleared, 1)

            def begin(st, use):
                wait_for(pe, drained[SLOT[use]], st.work(use) - 1)
                return bank(use)

            def turn_tiles(st, use, src):
                ps = begin(st, use)
                for i in range(TILES):
                    last = nc.tensor.transpose(ps[:, P * i:P * i + P], src[:, P * i:P * i + P], ident)
                last.then_inc(filled[SLOT[use]], 1)

            def three_passes(ps, w_a, w_b, x_a, x_b, start):
                mm(ps, w_a, x_a, start=start, stop=False, skip_group_check=True)
                mm(ps, w_a, x_b, start=False, stop=False, skip_group_check=True)
                return mm(ps, w_b, x_a, start=False, stop=True, skip_group_check=True)

            def piece(st, stage, what, k):
                uses = work_uses((stage, what, k))
                if what in ("keys", "queries", "values"):
                    x2 = ln["ln2"]
                    a = {"keys": WK, "queries": P * k, "values": WV}[what]
                    if what == "keys":
                        s = SLOT[("F", "turn", "ln2", 0)]
                        pe.wait_ge(drained[s], st.work_before(s))
                    ps = begin(st, uses[0])
                    three_passes(ps, w_hi[:, a:a + P], w_lo[:, a:a + P], x2["hi"][:, :], x2["lo"][:, :], True
                                 ).then_inc(filled[SLOT[uses[0]]], 1)
                elif what == "scores":
                    t, heads = SCORE_TILES[k]
                    n = KB * (t + 1)
                    if k == 0:
                        pe.wait_ge(q_done, st.upto("A", G, G))
                        pe.wait_ge(k_placed, st.upto("A", 1, 1))
                    ps = begin(st, uses[0])
                    for j, h in enumerate(heads):
                        mm(ps[:, n * j:n * j + n], q_rows[:, t, :, :], k_diag[:, 0:t + 1, h, :],
                           start=(j == 0), stop=False, skip_group_check=True)
                    diag = ps[:, 0:n * len(heads)].rearrange("p (j n) -> p j n", n=n)[:, :, n - KB:n]
                    mm(diag, mask_s[:, :], eye[:, :].unsqueeze(1).to_broadcast([P, len(heads), KB]),
                       start=False, stop=True, skip_group_check=True).then_inc(filled[SLOT[uses[0]]], 1)
                elif what == "probs":
                    if k == 0:
                        pe.wait_ge(m_in_rows, st.upto("A", 2 * 2 * G * 16, 2 * 2 * G * 16))
                    w = TOKENS - KB * k
                    for e, (u, gs, per) in enumerate(UNITS):
                        if u != k:
                            continue
                        wait_for(pe, exp_done, st.upto("A", len(UNITS), e - 1))
                        for j in range(2):
                            o = st_ps[:, e % 2, j, 0:per * w]
                            for i in range(per):
                                mm(o[:, w * i:w * i + w], k_diag[:, u, :, :], q_rows[:, u:BLOCKS, gs[j * per + i], :],
                                   start=(i == 0), stop=False, skip_group_check=True)
                            o = o.rearrange("p (i w) -> p i w", w=w)[:, :, 0:KB]
                            last = mm(o, mask_t[:, :], eye[:, :].unsqueeze(1).to_broadcast([P, per, KB]),
                                      start=False, stop=True, skip_group_check=True)
                        last.then_inc(st_filled, 1)
                elif what == "mix":
                    w = TOKENS - KB * k
                    pe.wait_ge(exp_done, st.upto("A", len(UNITS), UNITS_UPTO[k]))
                    if k == 0:
                        pe.wait_ge(v_done, st.upto("A", 1, 1))
                        wait_for(pe, num_out, st.upto("A", 1, 0))
                    for g in range(G):
                        last = mm(mix[KB * g:KB * g + KB, KB * k:TOKENS], v_diag[:, k, :], probs[:, k % PROBS_RING, g, 0:w],
                                  start=(k == 0), stop=(k == BLOCKS - 1), skip_group_check=True)
                    last.then_inc(mix_done, 1)
                elif what == "sums":
                    pe.wait_ge(sum_done, st.upto("B", ADDED, ADDED))
                    ps = begin(st, uses[0])
                    for g in range(G):
                        mm(ps[KB * g:KB * g + KB, :], par("block"), prob_sum[:, g, :], start=True, stop=False,
                           skip_group_check=True)
                    for u in range(ADDED, BLOCKS):
                        for g in range(G):
                            last = mm(ps[KB * g:KB * g + KB, KB * u:TOKENS], par("block"),
                                      probs[:, u % PROBS_RING, g, 0:TOKENS - KB * u], start=False, stop=(u == BLOCKS - 1),
                                      skip_group_check=True)
                    last.then_inc(filled[SLOT[uses[0]]], 1)
                elif what == "turn_out":
                    pe.wait_ge(num_out, st.upto("B", 1, 1))
                    turn_tiles(st, uses[0], num_t)
                    wait_drained(pe, st, ("B", "sums", 0, 0))
                    turn_tiles(st, uses[1], den_t)
                elif what == "turn":
                    L = ln[k]
                    pe.wait_ge(L["s_xn"], st.upto(stage, 1, 1))
                    turn_tiles(st, uses[0], L["xn"][:, :, :].rearrange("p i d -> p (i d)"))
                elif what == "hidden":
                    L, F = ln["ln1" if stage == "F" else "ln3"], ffn[stage]
                    if k == 0:
                        wait_low(st, "ln1" if stage == "F" else "ln3")
                    for j in range(2):
                        ps = begin(st, uses[j])
                        w = wgu_s[:, HIDDEN * j + P * k:HIDDEN * j + P * k + P]
                        mm(ps, w, L["hi"][:, :], start=True, stop=False)
                        mm(ps, w, L["lo"][:, :], start=False, stop=True).then_inc(filled[SLOT[uses[j]]], 1)
                elif what == "down":
                    F = ffn[stage]
                    pe.wait_ge(F["s_lo"], st.upto(stage, CHUNKS, CHUNKS))
                    ps = begin(st, uses[0])
                    for i in range(TILES):
                        for c in range(CHUNKS):
                            for part in ("hi", "lo"):
                                first, stop = (i == 0 and c == 0 and part == "hi"), (c == CHUNKS - 1 and part == "lo")
                                last = mm(ps[:, P * i:P * i + P], F[part][:, c, P * i:P * i + P], wd_s[:, P * c:P * c + P],
                                          start=first, stop=stop, skip_group_check=True)
                    last.then_inc(filled[SLOT[uses[0]]], 1)
                elif what == "out_proj":
                    L = ln["inner"]
                    wait_low(st, "inner")
                    ps = begin(st, uses[0])
                    for i in range(TILES):
                        o, t = ps[:, P * i:P * i + P], slice(P * i, P * i + P)
                        mm(o, L["hi"][:, t], wo_hi[:, :], start=(i == 0), stop=False, skip_group_check=True)
                        mm(o, L["hi"][:, t], wo_lo[:, :], start=False, stop=False, skip_group_check=True)
                        last = mm(o, L["lo"][:, t], wo_hi[:, :], start=False, stop=True, skip_group_check=True)
                    last.then_inc(filled[SLOT[uses[0]]], 1)

            def wait_low(st, name):
                wait_drained(pe, st, ("F" if name == "ln1" else "B", "turn", name, 0))

            run(pe, piece)

        @block.scalar
        def _(act):
            activate = nc.scalar.activation
            act.wait_ge(weights_ready, SETUP)

            def piece(st, stage, what, k):
                uses = work_uses((stage, what, k))
                if what in ("keys", "queries"):
                    if what == "keys":
                        i, scale, bias = 0, 1.0, par("bk")
                        wait_for(act, q_done, st.upto("A", G, 0))
                    else:
                        i, scale, bias = (k + 1) % 2, QSCALE, bq_s[:, k:k + 1]
                        if k == 1:
                            act.wait_ge(k_done, st.upto("A", 1, 1))
                        elif k > 1:
                            act.wait_ge(q_done, st.upto("A", G, k - 1))
                    wait_filled(act, st, uses[0])
                    activate(q_hi[:, i, :], bank(uses[0]), ACT.Identity, bias=bias, scale=scale).then_inc(q_high, 1)
                    activate(q_f[:, i, :], bank(uses[0]), ACT.Identity, bias=bias, scale=scale
                             ).then_inc(drained[SLOT[uses[0]]], 1)
                elif what == "values":
                    wait_filled(act, st, uses[0])
                    activate(v_turned[:, :], bank(uses[0]), ACT.Identity, bias=par("bv")).then_inc(drained[SLOT[uses[0]]], 1)
                elif what == "probs":
                    w = TOKENS - KB * k
                    wait_for(act, mix_done, st.upto("A", BLOCKS, k + 1 - PROBS_RING))
                    if k + 1 - PROBS_RING > 0:
                        act.wait_ge(sum_done, st.upto("A", ADDED, min(max(k + 1 - PROBS_RING, 2), ADDED)))
                    for e, (u, gs, per) in enumerate(UNITS):
                        if u != k:
                            continue
                        act.wait_ge(st_filled, st.upto("A", len(UNITS), e + 1))
                        o = probs[:, k % PROBS_RING, gs[0]:gs[-1] + 1, 0:w].rearrange("p (j i) w -> p j i w", i=per)
                        activate(o, st_ps[:, e % 2, :, 0:per * w].rearrange("p j (i w) -> p j i w", i=per), ACT.Exp
                                 ).then_inc(exp_done, 1)
                elif what == "sums":
                    act.wait_ge(mix_done, st.upto("B", BLOCKS, BLOCKS))
                    nc.scalar.copy(num_t[:, :], mix[:, :]).then_inc(num_out, 1)
                    wait_filled(act, st, uses[0])
                    nc.scalar.copy(den_t[:, :], bank(uses[0])).then_inc(drained[SLOT[uses[0]]], 1)
                elif what == "turn":
                    wait_filled(act, st, uses[0])
                    nc.scalar.copy(ln[k]["hi"][:, :], bank(uses[0])).then_inc(ln[k]["s_hi"], 1)
                elif what == "hidden":
                    F = ffn[stage]
                    wait_filled(act, st, uses[0])
                    activate(F["th"][:, k, :], bank(uses[0]), ACT.Tanh, scale=TANH_SCALE).then_inc(F["s_th"], 1)
                    wait_drained(act, st, uses[1])
                    nc.scalar.copy(F["hi"][:, k, :], F["h"][:, k, :]).then_inc(F["s_hi"], 1)

            run(act, piece)

        @block.vector
        def _(dve):
            v = nc.vector
            dve.wait_ge(params_loaded, 16)
            v.tensor_copy(w_hi[:, :], par("wqkv")).then_inc(w_high, 1)
            v.tensor_scalar(wo_g[:, :], par("wo"), par("ln_g"), None, ALU.mult).then_inc(wo_scaled, 1)
            v.tensor_copy(mask_s[:, :], par("mask_s")).then_inc(weights_ready, 1)
            v.tensor_copy(mask_t[:, :], par("mask_t")).then_inc(weights_ready, 1)
            v.tensor_copy(eye[:, :], par("eye")).then_inc(weights_ready, 1)
            v.tensor_scalar(bq_s[:, :], par("bq"), QSCALE, None, ALU.mult).then_inc(weights_ready, 1)
            dve.wait_ge(w_high, 1)
            v.tensor_tensor(w_lo[:, :], par("wqkv"), w_hi[:, :], ALU.subtract).then_inc(weights_ready, 1)
            dve.wait_ge(wo_scaled, 1)
            v.tensor_copy(wo_hi[:, :], wo_g[:, :]).then_inc(w_high, 1)
            dve.wait_ge(w_high, 2)
            v.tensor_tensor(wo_lo[:, :], wo_g[:, :], wo_hi[:, :], ALU.subtract).then_inc(weights_ready, 1)
            dve.wait_ge(bias_product, 1)
            v.tensor_tensor(bo_all[:, :], mix[:, 0:D], par("bo"), ALU.add).then_inc(weights_ready, 1)
            dve.wait_ge(ints_loaded, 32)
            v.tensor_scalar(wgu_s[:, :], wgu_i[:, :], WSCALE, None, ALU.mult).then_inc(weights_ready, 1)
            v.tensor_scalar(wd_s[:, :], wd_i[:, :], WSCALE, None, ALU.mult).then_inc(weights_ready, 1)
            dve.wait_ge(weights_ready, SETUP)
            dve.wait_ge(k_cleared, 1)

            def piece(st, stage, what, k):
                uses = work_uses((stage, what, k))
                if what in ("keys", "queries"):
                    wait_drained(dve, st, uses[0])
                    i = 0 if what == "keys" else (k + 1) % 2
                    o, low, s = ((k_rows[:, :].rearrange("p (u c) -> p u c", c=KB), par("low_k"), k_done)
                                 if what == "keys" else (q_rows[:, :, k, :], par("low_q"), q_done))
                    v.scalar_tensor_tensor(out=o, in0=q_hi[:, i, :].rearrange("p (u c) -> p u c", c=KB), scalar=low,
                                           in1=q_f[:, i, :].rearrange("p (u c) -> p u c", c=KB),
                                           op0=ALU.mult, op1=ALU.add).then_inc(s, 1)
                if what == "keys":
                    dve.wait_ge(k_done, st.upto("A", 1, 1))
                    for h in range(H):
                        r = slice(KB * h, KB * h + KB)
                        last = v.tensor_copy(k_diag[r, :, h, :], k_rows[r, :].rearrange("p (u c) -> p u c", c=KB))
                    last.then_inc(k_placed, 1)
                elif what == "values":
                    wait_drained(dve, st, uses[0])
                    v.transpose(v_diag[:, :, :].rearrange("p u c -> p (u c)"), v_turned[:, :]).then_inc(v_done, 1)
                elif what == "scores":
                    t, heads = SCORE_TILES[k]
                    n, nh = KB * (t + 1), len(heads)
                    wait_filled(dve, st, uses[0])
                    v.tensor_reduce(m_all[:, t // 8, heads[0]:heads[0] + nh, t % 8],
                                    bank(uses[0])[:, 0:n * nh].rearrange("p (j n) -> p j n", n=n), AX.X, ALU.max
                                    ).then_inc(drained[SLOT[uses[0]]], 1)
                elif what == "maxima":
                    last_tile = (FIRST_HALF if k == 0 else len(SCORE_TILES)) - 1
                    wait_drained(dve, st, ("A", "scores", last_tile, 0))
                    m = m_all[:, k, :, :].rearrange("p h t -> p (h t)")
                    v.tensor_copy(m_parts[:, k, 0, :], m).then_inc(m_high, 1)
                    dve.wait_ge(m_high, st.upto("A", 2, k + 1))
                    v.tensor_tensor(m_parts[:, k, 1, :], m, m_parts[:, k, 0, :], ALU.subtract).then_inc(m_split, 1)
                    dve.wait_ge(m_split, st.upto("A", 2, k + 1))
                    wait_for(dve, m_in_rows, st.upto("A", 4 * G * 16, 0))
                    v.transpose(m_turned[:, k, :, :].rearrange("p a c -> p (a c)"),
                                m_parts[:, k, :, :].rearrange("p a c -> p (a c)")).then_inc(m_turn, 1)
                elif what == "carry":
                    v.tensor_tensor(x_mid[:, :, :], x_front[:, :, :], bo_all[:, :].unsqueeze(1).to_broadcast([P, TILES, D]),
                                    ALU.add).then_inc(x_mid_done, 1)
                elif what == "turn_out":
                    wait_filled(dve, st, uses[1])
                    v.reciprocal(rden[:, :], bank(uses[1]).rearrange("p (c d) -> p c d", d=HD)[:, :, 0]
                                 ).then_inc(drained[SLOT[uses[1]]], 1)
                    wait_drained(dve, st, uses[1])
                    v.tensor_tensor(attended[:, :, :].rearrange("p i (c d) -> p (i c) d", d=HD),
                                    bank(uses[0]).rearrange("p (c d) -> p c d", d=HD),
                                    rden[:, :].unsqueeze(2).to_broadcast([P, TILES * G * H, HD]), ALU.mult
                                    ).then_inc(drained[SLOT[uses[0]]], 1)
                elif what == "stats":
                    L = ln[k]
                    if k == "ln1":
                        dve.wait_ge(x_loaded, st.upto("F", 16, 16))
                    else:
                        wait_drained(dve, st, {"ln2": ("F", "down", 0, 0), "inner": ("B", "turn_out", 0, 0),
                                               "ln3": ("B", "out_proj", 0, 0)}[k])
                    for i in range(TILES):
                        v.bn_stats(L["bn"][:, i, :], L["src"][:, i, :]).then_inc(L["s_bn"], 1)
                    dve.wait_ge(L["s_bn"], st.upto(stage, TILES, TILES))
                    v.memset(gate[:, :], 0.0)
                    for i in range(TILES):
                        v.bn_aggr(L["mv"][:, i, :], L["bn"][:, i, :]).then_inc(L["s_mv"], 1)
                elif what == "norm":
                    L = ln[k]
                    dve.wait_ge(L["s_rstd"], st.upto(stage, 1, 1))
                    for i in range(TILES):
                        last = v.tensor_scalar(L["xn"][:, i, :], L["src"][:, i, :], L["mv"][:, i, 0:1], L["rstd"][:, i:i + 1],
                                               ALU.subtract, ALU.mult)
                    last.then_inc(L["s_xn"], 1)
                elif what == "turn":
                    L = ln[k]
                    dve.wait_ge(L["s_hi"], st.upto(stage, 1, 1))
                    v.tensor_tensor(L["lo"][:, :], bank(uses[0]), L["hi"][:, :], ALU.subtract
                                    ).then_inc(drained[SLOT[uses[0]]], 1)
                elif what == "hidden":
                    F = ffn[stage]
                    dve.wait_ge(F["s_th"], st.upto(stage, CHUNKS, k + 1))
                    v.scalar_tensor_tensor(out=F["a"][:, k, :], in0=F["th"][:, k, :], scalar=1.0, in1=bank(uses[0]),
                                           op0=ALU.add, op1=ALU.mult).then_inc(drained[SLOT[uses[0]]], 1)
                    wait_filled(dve, st, uses[1])
                    wait_drained(dve, st, uses[0])
                    v.tensor_tensor(F["h"][:, k, :], F["a"][:, k, :], bank(uses[1]), ALU.mult
                                    ).then_inc(drained[SLOT[uses[1]]], 1)
                elif what == "down":
                    wait_filled(dve, st, uses[0])
                    if stage == "B":
                        dve.wait_ge(y_free, 16 + st.upto("B", 16, 0))
                    elif "A" in st.stages:
                        dve.wait_ge(x_mid_done, st.upto("A", 1, 1))
                    o, res = (x_front, x_in) if stage == "F" else (y, x_att)
                    v.scalar_tensor_tensor(out=flat(o), in0=bank(uses[0]), scalar=FFN_SCALE, in1=flat(res),
                                           op0=ALU.mult, op1=ALU.add).then_inc(drained[SLOT[uses[0]]], 1)
                elif what == "out_proj":
                    wait_filled(dve, st, uses[0])
                    dve.wait_ge(x_mid_done, st.upto("B", 1, 1))
                    v.tensor_tensor(flat(x_att), bank(uses[0]), flat(x_mid), ALU.add).then_inc(drained[SLOT[uses[0]]], 1)

            def flat(t):
                return t[:, :, :].rearrange("p i d -> p (i d)")

            run(dve, piece)

        @block.gpsimd
        def _(pool):
            g_ = nc.gpsimd
            g_.memset(k_diag[:, :, :, :], 0.0).then_inc(k_cleared, 1)
            g_.memset(y[:, 0, 0:1], 0.0).then_inc(y_free, 16)
            pool.wait_ge(weights_ready, SETUP)

            def piece(st, stage, what, k):
                uses = work_uses((stage, what, k))
                if what == "mix" and k < ADDED:
                    w = TOKENS - KB * k
                    pool.wait_ge(exp_done, st.upto("A", len(UNITS), UNITS_UPTO[k]))
                    e = probs[:, k % PROBS_RING, :, 0:w]
                    if k == 0:
                        if "B" in st.stages:
                            wait_filled(pool, st, ("B", "sums", 0, 0))
                        g_.tensor_tensor(prob_sum[:, :, 0:KB], e[:, :, 0:KB],
                                         par("zero").unsqueeze(2).to_broadcast([P, G, KB]), ALU.add).then_inc(sum_done, 1)
                    elif k == 1:
                        g_.tensor_tensor(prob_sum[:, :, KB:TOKENS], probs[:, 0, :, KB:TOKENS], e, ALU.add).then_inc(sum_done, 1)
                    else:
                        pool.wait_ge(sum_done, st.upto("A", ADDED, k))
                        o = prob_sum[:, :, KB * k:TOKENS]
                        g_.tensor_tensor(o, o, e, ALU.add).then_inc(sum_done, 1)
                elif what == "stats":
                    L = ln[k]
                    pool.wait_ge(L["s_mv"], st.upto(stage, TILES, TILES))
                    g_.tensor_tensor(L["var"][:, :], L["mv"][:, :, 1], par("eps"), ALU.add).then_inc(L["s_var"], 1)
                    pool.wait_ge(L["s_var"], st.upto(stage, 1, 1))
                    g_.tensor_tensor(L["rstd"][:, :], L["var"][:, :], par("neg_half"), ALU.pow).then_inc(L["s_rstd"], 1)
                elif what == "hidden":
                    F = ffn[stage]
                    pool.wait_ge(F["s_hi"], st.upto(stage, CHUNKS, k + 1))
                    g_.tensor_tensor(F["lo"][:, k, :], F["h"][:, k, :], F["hi"][:, k, :], ALU.subtract).then_inc(F["s_lo"], 1)

            run(pool, piece)

    return nc


def layout(inputs):
    f = {n[len("L0_attn_"):]: np.asarray(a) for n, a in inputs.items() if n.startswith("L0_attn_")}
    one = np.float32

    def rows(w, keep):
        o = np.zeros(w.shape[:-2] + (H, 4, HD), one)
        for slot in range(3):
            o[..., slot, :] = w
        return o.reshape(keep + (-1,))

    wq, wk = rows(f["Wq"].reshape(D, G, H, HD), (D,)), rows(f["Wk"].reshape(D, H, HD), (D,))
    bq = rows(f["bq"].reshape(G, H, HD), (G,)).T
    wv, bv = np.zeros((D, H, H, HD), one), np.zeros((H, H, HD), one)
    for h in range(H):
        wv[:, h, h], bv[h, h] = f["Wv"][:, HD * h:HD * h + HD], f["bv"][HD * h:HD * h + HD]
    bk = rows(f["bk"].reshape(H, HD), ())
    bk = bk.reshape(H, 4, HD)
    bk[:, 3, 0:2] = -1.0
    row = np.arange(P)
    slot = (row // HD) % 4
    a, k = np.arange(P)[:, None], np.arange(P)[None, :] % KB
    cols = {
        "wqkv": np.concatenate([wq, wk, wv.reshape(D, P)], 1), "wo": f["Wo"], "ln_b": np.repeat(f["ln_b"][:, None], P, 1),
        "bo": np.repeat(f["bo"][None], P, 0), "bv": bv.reshape(P, 1), "bq": bq, "bk": bk.reshape(P, 1),
        "ln_g": f["ln_g"][:, None], "ident": np.eye(P, dtype=one),
        "mask_s": np.where((a < KB) & (a > k), one(MASKED), one(0)),
        "mask_t": np.where((a < KB) & (a < k), one(MASKED), one(0)),
        "eye": np.eye(P, KB, dtype=one), "block": (row[:, None] // KB == np.arange(H * HD)[None] // HD).astype(one),
        "low_q": np.where(slot == 2, one(-1), one(0))[:, None], "low_k": np.where(slot == 1, one(-1), one(0))[:, None],
        "neg_half": np.full((P, TILES), -0.5, one), "eps": np.full((P, TILES), EPS, one),
        "zero": np.zeros((P, 1), one),
    }
    packed = np.empty((P, PACKED), one)
    for name, (lo, hi) in PACK.items():
        packed[:, lo:hi] = cols[name]
    wg, wu, wd = (np.asarray(inputs["L0_ffn_" + n]) for n in ("w_gate", "w_up", "w_down"))
    wgu = np.ascontiguousarray(np.concatenate([wg, wu], 0).T)
    wd = np.ascontiguousarray(wd.T.reshape(CHUNKS, P, D).transpose(1, 0, 2).reshape(P, HIDDEN))
    return np.ascontiguousarray(f["x"]), packed, wgu, wd


def kernel(**inputs):
    import concourse.bacc as bacc
    from concourse.bass_utils import run_bass_kernel_spmd

    nc = bacc.Bacc("TRN2", target_bir_lowering=False, num_devices=1)
    arrays, args = {}, []
    for name, a in zip(("x", "packed", "wgu", "wd"), layout(inputs)):
        arrays[name] = a
        args.append(nc.dram_tensor(name, a.shape, mybir.dt.from_np(a.dtype), kind="ExternalInput").ap())
    out = nc.dram_tensor("out", (ENTRIES, TOKENS, D), F32, kind="ExternalOutput").ap()
    macaron(nc, *args, out)
    r = run_bass_kernel_spmd(nc, [arrays], core_ids=[0])
    return r.results[0]["out"]
```

```python
from contextlib import ExitStack

import numpy as np

import concourse.bass as bass
from concourse import mybir

F32 = mybir.dt.float32
F16 = mybir.dt.float16
BF16 = mybir.dt.bfloat16
I32 = mybir.dt.int32
ALU = mybir.AluOpType
ACT = mybir.ActivationFunctionType
AX = mybir.AxisListType

P = 128
ENTRIES, TOKENS, D = 8, 512, 128
TILES = TOKENS // P
G, H, HD = 4, 4, 8
KB = 32
BLOCKS = TOKENS // KB
CHUNKS = 3
HIDDEN = CHUNKS * P
LAST_CHUNK = CHUNKS - 1
EPS = 1e-5
WSCALE = 2.0 ** -7
QSCALE = float(HD) ** -0.5
TANH_SCALE = 0.5 * 128.0 / 127.0
FFN_SCALE = 0.25 * (128.0 / 127.0) ** 3
MASKED = -1e30
PROBS_RING = 8
ADDED = 11

PACK = {}
_at = 0
for _name, _n in (("wqkv", G * P + 2 * P), ("wo", D), ("ln_b", P), ("bo", D),
                  ("bq", G), ("bk", 1), ("bv", 1), ("ln_g", 1), ("ident", P), ("mask_s", P), ("mask_t", P),
                  ("eye", KB), ("block", H * HD), ("low_q", 1), ("low_k", 1), ("neg_half", TILES), ("eps", TILES), ("minus_one", TILES), ("zero", 1)):
    PACK[_name] = (_at, _at + _n)
    _at += _n
PACKED = _at


SCORE_TILES = [(t, tuple(range(h, h + n))) for t in range(BLOCKS)
               for n in ((4 if t < 4 else 2 if t < 8 else 1),) for h in range(0, H, n)]
FIRST_HALF = sum(t < BLOCKS // 2 for t, _ in SCORE_TILES)


ST_BANKS = 2
UNITS = [(u, g, n) for u in range(BLOCKS) for n in (1 if TOKENS - KB * u > 256 else 2 if TOKENS - KB * u > 128 else 4,)
         for g in range(0, G, n)]
assert len(UNITS) % ST_BANKS == 0
UNITS_UPTO = [sum(1 for v, _, _ in UNITS if v <= u) for u in range(BLOCKS)]


ORDERS = {
    "F": """
        F.stats.ln1 F.norm.ln1 F.turn.ln1 F.hidden.0 F.gated.0 F.hidden.1 F.gated.1 F.hidden.2 F.gated.2 F.down.0
        F.down.1 F.down.2 F.stats.ln2 F.norm.ln2 F.turn.ln2 F.carry.0
    """,
    "FS": """
        F.stats.ln1 S.keys.0 S.queries.0 S.queries.1 S.queries.2 S.queries.3 S.scores.0 S.scores.1 S.scores.2 S.scores.3
        S.scores.4 S.scores.5 S.scores.6 F.norm.ln1 F.turn.ln1 S.scores.7 S.scores.8 S.values.0 F.hidden.0 S.scores.9
        S.scores.10 S.scores.11 S.scores.12 S.maxima.0 S.scores.13 S.scores.14 S.scores.15 S.scores.16 S.scores.17
        S.scores.18 S.scores.19 S.scores.20 S.scores.21 F.gated.0 S.scores.22 S.scores.23 S.scores.24 S.scores.25
        F.hidden.1 F.gated.1 F.hidden.2 S.scores.26 S.scores.27 F.gated.2 S.scores.28 S.scores.29 F.down.0 F.down.1
        F.down.2 F.stats.ln2 S.scores.30 S.scores.31 S.scores.32 S.scores.33 S.scores.34 S.scores.35 S.scores.36
        F.norm.ln2 S.scores.37 F.turn.ln2 S.scores.38 S.scores.39 S.scores.40 S.scores.41 S.scores.42 F.carry.0
        S.scores.43 S.maxima.1
    """,
    "FSP": """
        F.stats.ln1 S.keys.0 S.queries.0 S.values.0 S.queries.1 S.queries.2 S.queries.3 P.probs.0 S.scores.0 S.scores.1
        S.scores.2 P.probs.2 S.scores.3 F.norm.ln1 S.scores.4 S.scores.5 S.scores.6 P.probs.4 S.scores.7 S.scores.8
        S.scores.9 S.scores.10 P.probs.6 F.turn.ln1 P.probs.8 P.add.0 P.add.1 S.scores.11 P.mix.0 P.mix.1 P.probs.10
        S.scores.12 P.probs.12 S.maxima.0 S.scores.13 P.add.2 F.hidden.0 F.gated.0 P.probs.14 P.mix.2 P.probs.16
        S.scores.14 S.scores.15 S.scores.16 P.probs.18 S.scores.17 P.add.3 F.hidden.1 S.scores.18 P.probs.20 S.scores.19
        F.gated.1 P.probs.22 S.scores.20 S.scores.21 P.probs.24 P.probs.26 P.mix.3 P.probs.28 S.scores.22 S.scores.23
        P.probs.30 P.probs.32 S.scores.24 S.scores.25 F.hidden.2 S.scores.26 S.scores.27 S.scores.28 P.add.4 P.add.5
        P.add.6 P.probs.34 S.scores.29 F.gated.2 F.down.0 S.scores.30 S.scores.31 F.down.1 F.down.2 F.stats.ln2
        S.scores.32 P.mix.4 S.scores.33 P.mix.5 P.mix.6 P.mix.7 P.mix.8 S.scores.34 S.scores.35 P.probs.36 S.scores.36
        F.norm.ln2 P.add.7 P.add.8 S.scores.37 S.scores.38 P.probs.38 S.scores.39 F.turn.ln2 P.probs.40 S.scores.40
        S.scores.41 P.add.9 P.mix.9 P.add.10 P.mix.10 P.probs.42 P.mix.11 S.scores.42 S.scores.43 F.carry.0 P.mix.12
        P.mix.13 P.mix.14 S.maxima.1 P.mix.15
    """,
    "FSPB": """
        S.keys.0 S.queries.0 S.values.0 S.queries.1 S.queries.2 F.stats.ln1 B.sums.0 B.sums.1 S.queries.3 B.turn_out.0
        P.probs.0 P.probs.2 S.scores.0 B.stats.inner S.scores.1 P.probs.4 F.norm.ln1 P.mix.0 P.add.0 S.scores.2
        S.scores.3 P.probs.6 S.scores.4 S.scores.5 S.scores.6 S.scores.7 S.scores.8 B.norm.inner P.probs.8 P.add.1
        S.scores.9 B.turn.inner S.scores.10 P.probs.10 S.scores.11 F.turn.ln1 P.probs.12 P.add.2 P.mix.1 S.scores.12
        S.scores.13 P.probs.14 F.hidden.0 S.scores.14 S.scores.15 P.probs.16 F.gated.0 B.out_proj.0 S.scores.16
        S.scores.17 P.add.3 P.probs.18 F.hidden.1 F.gated.1 P.probs.20 S.scores.18 S.scores.19 P.mix.2 B.stats.ln3
        F.hidden.2 P.probs.22 P.mix.3 S.scores.20 S.scores.21 P.probs.24 F.down.0 P.probs.26 S.maxima.0 S.scores.22
        S.scores.23 F.down.1 S.scores.24 P.mix.4 P.add.4 F.gated.2 S.scores.25 B.norm.ln3 S.scores.26 B.turn.ln3
        P.probs.28 F.down.2 S.scores.27 S.scores.28 P.probs.30 P.add.5 B.hidden.0 B.gated.0 S.scores.29 F.stats.ln2
        P.probs.32 S.scores.30 B.hidden.1 P.probs.34 S.scores.31 P.mix.5 P.mix.6 P.add.6 P.add.7 S.scores.32 P.mix.7
        S.scores.33 P.probs.36 S.scores.34 P.mix.8 B.gated.1 P.mix.9 P.probs.38 S.scores.35 S.scores.36 F.carry.0
        B.hidden.2 P.probs.40 S.scores.37 P.mix.10 S.scores.38 P.mix.11 F.norm.ln2 S.scores.39 B.gated.2 P.add.8
        P.mix.12 P.mix.13 P.probs.42 B.down.0 S.scores.40 S.scores.41 F.turn.ln2 P.mix.14 B.down.1 S.scores.42 P.mix.15
        S.scores.43 S.maxima.1 P.add.9 P.add.10 B.down.2
    """,
    "SPB": """
        S.keys.0 S.queries.0 S.values.0 S.queries.1 B.sums.0 S.queries.2 S.queries.3 B.sums.1 P.probs.0 B.turn_out.0
        B.stats.inner S.scores.0 S.scores.1 P.probs.2 P.probs.4 P.probs.6 S.scores.2 S.scores.3 P.probs.8 S.scores.4
        P.probs.10 B.norm.inner S.scores.5 S.scores.6 S.scores.7 S.scores.8 P.probs.12 S.scores.9 S.scores.10 P.probs.14
        S.scores.11 S.scores.12 B.turn.inner P.mix.0 S.scores.13 P.add.0 P.add.1 P.probs.16 P.add.2 S.maxima.0 P.mix.1
        S.scores.14 P.mix.2 P.probs.18 B.out_proj.0 P.add.3 S.scores.15 P.probs.20 P.probs.22 S.scores.16 P.probs.24
        P.mix.3 B.stats.ln3 P.probs.26 S.scores.17 P.add.4 P.add.5 S.scores.18 P.mix.4 S.scores.19 S.scores.20
        S.scores.21 P.add.6 P.mix.5 S.scores.22 B.norm.ln3 P.mix.6 P.probs.28 S.scores.23 S.scores.24 P.probs.30
        S.scores.25 S.scores.26 B.turn.ln3 S.scores.27 S.scores.28 P.probs.32 P.probs.34 S.scores.29 B.hidden.0
        S.scores.30 S.scores.31 B.gated.0 P.mix.7 P.mix.8 S.scores.32 S.scores.33 B.hidden.1 S.scores.34 S.scores.35
        P.add.7 P.mix.9 S.scores.36 S.scores.37 P.probs.36 S.scores.38 P.add.8 S.scores.39 S.scores.40 P.probs.38
        B.gated.1 S.scores.41 P.probs.40 S.scores.42 B.down.0 S.scores.43 S.maxima.1 P.add.9 P.add.10 B.hidden.2
        P.mix.10 P.probs.42 P.mix.11 P.mix.12 P.mix.13 B.gated.2 P.mix.14 B.down.1 B.down.2 P.mix.15
    """,
    "PB": """
        B.sums.0 B.sums.1 B.turn_out.0 B.stats.inner P.probs.0 P.probs.2 P.probs.4 P.probs.6 P.probs.8 P.mix.0
        P.probs.10 P.probs.12 P.probs.14 P.mix.1 P.mix.2 P.add.0 B.norm.inner B.turn.inner P.probs.16 P.probs.18 P.mix.3
        P.add.1 P.add.2 P.mix.4 P.probs.20 P.probs.22 B.out_proj.0 P.mix.5 P.add.3 P.add.4 B.stats.ln3 P.add.5
        P.probs.24 P.probs.26 P.probs.28 P.probs.30 P.probs.32 P.mix.6 P.mix.7 P.mix.8 B.norm.ln3 B.turn.ln3 P.add.6
        P.add.7 P.probs.34 P.probs.36 B.hidden.0 B.gated.0 P.probs.38 B.hidden.1 B.gated.1 P.probs.40 B.hidden.2
        P.probs.42 P.mix.9 P.mix.10 P.mix.11 P.mix.12 P.mix.13 P.mix.14 P.mix.15 P.add.8 P.add.9 B.down.0 B.down.1
        B.gated.2 B.down.2 P.add.10
    """,
    "B": """
        B.sums.0 B.sums.1 B.turn_out.0 B.stats.inner B.norm.inner B.turn.inner B.out_proj.0 B.stats.ln3 B.norm.ln3
        B.turn.ln3 B.hidden.0 B.gated.0 B.hidden.1 B.gated.1 B.hidden.2 B.gated.2 B.down.0 B.down.1 B.down.2
    """,
}


def pieces(kind):
    split = (word.split(".") for word in ORDERS[kind].split())
    return [(stage, what, int(k) if k.isdigit() else k) for stage, what, k in split]


def work_uses(item):
    stage, what, k = item
    n = {"keys": 1, "queries": 1, "values": 1, "scores": 1, "sums": 1, "turn_out": 2, "turn": 1,
         "hidden": 2, "down": 1, "out_proj": 1}.get(what, 0)
    if what in ("sums", "down") and k > 0:
        n = 0
    return [(stage, what, k, j) for j in range(n)]


SCORE_BANKS, OTHER_BANKS = 2, 3
UP_ON_GPSIMD = (("F", 0), ("B", 0))
UPS = {stage: [k for s, k in UP_ON_GPSIMD if s == stage] for stage in "FB"}
WORK = SCORE_BANKS + OTHER_BANKS
STAGES = "FSPB"
NORM_ON_SCALAR = ("ln1", "ln2", "inner", "ln3")


class Plan:

    def __init__(self, order):
        self.items = order
        uses = [u for item in order for u in work_uses(item)]
        scores = [u for u in uses if u[1] == "scores"]
        others = [u for u in uses if u[1] != "scores"]
        shift = others.index(LN2_TURN) if LN2_TURN in others else 0
        self.slot = {u: i % SCORE_BANKS for i, u in enumerate(scores)}
        self.slot.update({u: SCORE_BANKS + (i - shift) % OTHER_BANKS for i, u in enumerate(others)})
        self.fills, self.rank = [0] * WORK, {}
        for u in uses:
            self.fills[self.slot[u]] += 1
            self.rank[u] = self.fills[self.slot[u]]


LN2_TURN = ("F", "turn", "ln2", 0)
PLANS = {kind: Plan(pieces(kind)) for kind in ORDERS}


class Step:

    LEAD = {"F": 2, "S": 1, "P": 0, "B": -1}

    def __init__(self, b, parity):
        self.b, self.parity = b, parity
        self.before = {stage: b + lead for stage, lead in self.LEAD.items()}
        self.stages = STAGES
        if isinstance(b, int):
            self.stages = self.kind(b)
            self.before = {stage: min(max(n, 0), ENTRIES) for stage, n in self.before.items()}

        self.plan = PLANS[self.stages]

    def kind(self, b):
        return "".join(stage for stage in STAGES if 0 <= b + self.LEAD[stage] < ENTRIES)

    def upto(self, stage, per, k):
        return self.before[stage] * per + k

    def slot(self, use):
        return self.plan.slot[use]

    def work(self, use):
        return self.work_before(self.slot(use)) + self.plan.rank[use]

    def work_before(self, slot):
        if isinstance(self.b, int):
            return sum(PLANS[self.kind(b)].fills[slot] for b in range(-2, self.b))
        full = PLANS[STAGES].fills[slot]
        return self.b * full + (sum(PLANS[self.kind(b)].fills[slot] for b in range(-2, 1)) - full)


def wait_for(eng, sem, value):
    if not isinstance(value, int) or value > 0:
        eng.wait_ge(sem, value)


def macaron(nc, x, packed, wgu, wd, out):
    x_v = x.rearrange("e (i p) d -> e p i d", p=P)
    out_v = out.rearrange("e (i p) d -> e p i d", p=P)
    with ExitStack() as ctx:
        def sb(name, shape, dt=F32):
            return ctx.enter_context(nc.sbuf_tensor(name, [P] + shape, dt))

        def sem(name):
            return ctx.enter_context(nc.semaphore(name))

        params = sb("params", [PACKED])

        def par(name):
            a, z = PACK[name]
            return params[:, a:z]

        wgu_i = sb("wgu_i", [2 * HIDDEN], I32)
        wd_i = sb("wd_i", [HIDDEN], I32)
        wgu_s = sb("wgu_s", [2 * HIDDEN], F16)
        wd_s = sb("wd_s", [HIDDEN])
        NQKV = G * P + 2 * P
        w_hi = sb("w_hi", [NQKV], F16)
        w_lo = sb("w_lo", [NQKV], F16)
        wo_g = sb("wo_g", [D])
        wo_hi = sb("wo_hi", [D], F16)
        wo_lo = sb("wo_lo", [D], F16)
        bo_all = sb("bo_all", [D])
        bq_s = sb("bq_s", [G])
        mask_s = sb("mask_s_b", [P], BF16)
        mask_t = sb("mask_t_b", [P], BF16)
        eye = sb("eye_b", [KB], BF16)
        ident = par("ident")
        WK, WV = G * P, G * P + P

        x_in = sb("x_in", [TILES, D])
        x_front = sb("x_front", [TILES, D])
        x_mid = sb("x_mid", [ENTRIES, TILES, D])
        x_att = sb("x_att", [TILES, D])
        y = sb("y", [TILES, D])
        ln = {}
        for name in ("ln1", "ln2", "inner", "ln3"):
            ln[name] = dict(
                bn=sb(f"{name}_bn", [TILES, 6]), mv=sb(f"{name}_mv", [TILES, 2]), rstd=sb(f"{name}_rstd", [TILES]),
                var=sb(f"{name}_var", [TILES]), s_var=sem(f"{name}_var_eps"),
                minus=sb(f"{name}_minus_rstd", [TILES]), s_minus=sem(f"{name}_minus_rstd_ready"),
                shift=sb(f"{name}_shift", [TILES]), s_shift=sem(f"{name}_shift_ready"),
                xn=sb(f"{name}_xn", [TILES, D]), hi=sb(f"{name}_hi", [TOKENS], F16), lo=sb(f"{name}_lo", [TOKENS], F16),
                s_bn=sem(f"{name}_tile_stats"), s_mv=sem(f"{name}_moments"), s_rstd=sem(f"{name}_rstd_ready"),
                s_xn=sem(f"{name}_normalised"), s_hi=sem(f"{name}_high_part"))
        gate = sb("gate", [1])
        attended = sb("attended", [TILES, D])
        ln["ln1"]["src"], ln["ln2"]["src"], ln["inner"]["src"], ln["ln3"]["src"] = x_in, x_front, attended, x_att
        ffn = {}
        for st in "FB":
            ffn[st] = dict(
                th=sb(f"{st}_th", [2, TOKENS]), h=sb(f"{st}_h", [CHUNKS, TOKENS]),
                up=sb(f"{st}_up", [CHUNKS, TOKENS]), s_h=sem(f"{st}_hidden_ready"),
                s_th=sem(f"{st}_tanh_ready"))
        q_hi = sb("q_hi", [2, TOKENS], F16)
        q_f = sb("q_f", [2, TOKENS])
        q_rows = sb("q_rows", [2, BLOCKS, G, KB], F16)
        k_rows = sb("k_rows", [TOKENS], F16)
        k_diag = sb("k_diag", [2, BLOCKS, H, KB], F16)
        v_turned = sb("v_turned", [TOKENS])
        v_diag = sb("v_diag", [2, BLOCKS, H * HD])
        m_all = sb("m_all", [2, H, 8])
        m_parts = sb("m_parts", [2, 2, KB], F16)
        m_turned = sb("m_turned", [2, 2, KB], F16)
        probs = sb("probs", [PROBS_RING, G, TOKENS])
        prob_sum = sb("prob_sum", [G, TOKENS])
        num_t = sb("num_t", [TOKENS])
        den_t = sb("den_t", [TOKENS])
        rden = sb("rden", [TILES * G * H])

        work = ctx.enter_context(nc.psum_tensor("work", [P, WORK, 512], F32))
        mix = ctx.enter_context(nc.psum_tensor("mix", [P, 512], F32))
        st_ps = ctx.enter_context(nc.psum_tensor("st_ps", [P, ST_BANKS, 512], F32))

        def bank(st, use):
            return work[:, st.slot(use), :]

        params_loaded, ints_loaded, x_loaded, y_free = sem("params_loaded"), sem("ints_loaded"), sem("x_loaded"), sem("y_free")
        weights_ready, wo_scaled, w_high, bias_product = sem("weights_ready"), sem("wo_scaled"), sem("w_high"), sem("bias_product")
        k_cleared = sem("k_diag_cleared")
        filled = [sem(f"work{s}_filled") for s in range(WORK)]
        drained = [sem(f"work{s}_drained") for s in range(WORK)]
        q_high, q_done, k_done, k_placed = sem("q_high"), sem("q_rows_ready"), sem("k_rows_ready"), sem("k_diag_ready")
        v_done = sem("v_diag_ready")
        m_high, m_split, m_turn, m_in_rows = sem("m_high"), sem("m_split"), sem("m_turned_ready"), sem("m_in_q_rows")
        st_filled, exp_done, mix_done, sum_done = sem("st_filled"), sem("exp_done"), sem("mix_done"), sem("prob_sum_done")
        num_out = sem("num_out")
        x_mid_done = sem("x_mid_done")
        SETUP = 9

        block = ctx.enter_context(nc.Block())

        def run(eng, piece):
            for b in range(-2, 1):
                step(eng, piece, Step(b, b % 2))
            with eng.Fori(1, 4, 2) as b:
                step(eng, piece, Step(b, 1))
                step(eng, piece, Step(b + 1, 0))
            for b in range(5, ENTRIES + 1):
                step(eng, piece, Step(b, b % 2))

        def st_tile(st, e):
            u, _, n = UNITS[e]
            w = TOKENS - KB * u
            return st_ps[:, e % ST_BANKS, 0:n * w].rearrange("p (j w) -> p j w", w=w)

        def step(eng, piece, st):
            for item in st.plan.items:
                piece(st, *item)

        def wait_drained(eng, st, use):
            eng.wait_ge(drained[st.slot(use)], st.work(use))

        def wait_filled(eng, st, use):
            eng.wait_ge(filled[st.slot(use)], st.work(use))

        def entry(t, e):
            return t[:, e] if isinstance(e, int) else t[:, bass.ds(e, 1)].rearrange("p e i d -> p (e i) d")

        @block.sync
        def _(sp):
            sp.dma_start(x_in[:, :, :], x_v[0]).then_inc(x_loaded, 16)
            sp.dma_start(params[:, :], packed).then_inc(params_loaded, 16)
            sp.dma_start(wgu_i[:, :], wgu).then_inc(ints_loaded, 16)
            sp.dma_start(wd_i[:, :], wd).then_inc(ints_loaded, 16)

            def piece(st, stage, what, k):
                if (stage, what, k) == ("F", "down", LAST_CHUNK) and (not isinstance(st.b, int) or st.b + 3 < ENTRIES):
                    wait_drained(sp, st, (stage, what, 0, 0))
                    sp.dma_start(x_in[:, :, :], x_v[bass.ds(st.b + 3, 1)].rearrange("a p i d -> p (a i) d")
                                 ).then_inc(x_loaded, 16)
                if what == "maxima":
                    sp.wait_ge(m_turn, st.upto("S", 2, k + 1))
                    for g in range(G):
                        for part in range(2):
                            row = 3 * HD + part
                            sp.dma_start(
                                q_rows[row:row + 3 * KB + 1:KB, 1 - st.parity, 8 * k:8 * k + 8, g, :],
                                m_turned[KB * g:KB * g + KB, k, part, :]).then_inc(m_in_rows, 16)
                if (stage, what, k) == ("B", "down", LAST_CHUNK):
                    wait_drained(sp, st, (stage, what, 0, 0))
                    sp.dma_start(out_v[bass.ds(st.b - 1, 1)].rearrange("a p i d -> p (a i) d"), y[:, :, :]
                                 ).then_inc(y_free, 16)

            run(sp, piece)
            sp.wait_ge(y_free, 16 + 16 * ENTRIES)

        @block.tensor
        def _(pe):
            mm = nc.tensor.matmul
            pe.wait_ge(params_loaded, 16)
            mm(mix[:, 0:D], par("ln_b"), par("wo"), start=True, stop=True).then_inc(bias_product, 1)
            pe.wait_ge(weights_ready, SETUP)
            pe.wait_ge(k_cleared, 1)

            def begin(st, use, after=None):
                if after and st.slot(after) != st.slot(use):
                    wait_drained(pe, st, after)
                wait_for(pe, drained[st.slot(use)], st.work(use) - 1)
                return bank(st, use)

            def turn_tiles(st, use, src, after=None):
                ps = begin(st, use, after)
                for i in range(TILES):
                    last = nc.tensor.transpose(ps[:, P * i:P * i + P], src[:, P * i:P * i + P], ident)
                last.then_inc(filled[st.slot(use)], 1)

            def three_passes(ps, w_a, w_b, x_a, x_b, start):
                mm(ps, w_a, x_a, start=start, stop=False, skip_group_check=True)
                mm(ps, w_a, x_b, start=False, stop=False, skip_group_check=True)
                return mm(ps, w_b, x_a, start=False, stop=True, skip_group_check=True)

            def piece(st, stage, what, k):
                uses = work_uses((stage, what, k))
                if what in ("keys", "queries", "values"):
                    x2 = ln["ln2"]
                    a = {"keys": WK, "queries": P * k, "values": WV}[what]
                    if what == "keys":
                        s = PLANS["FSPB"].slot[LN2_TURN]
                        if st.slot(uses[0]) != s:
                            pe.wait_ge(drained[s], st.work_before(s))
                    ps = begin(st, uses[0])
                    three_passes(ps, w_hi[:, a:a + P], w_lo[:, a:a + P], x2["hi"][:, :], x2["lo"][:, :], True
                                 ).then_inc(filled[st.slot(uses[0])], 1)
                elif what == "scores":
                    t, heads = SCORE_TILES[k]
                    n = KB * (t + 1)
                    if k == 0:
                        pe.wait_ge(q_done, st.upto("S", G, G))
                        pe.wait_ge(k_placed, st.upto("S", 1, 1))
                    ps = begin(st, uses[0])
                    for j, h in enumerate(heads):
                        mm(ps[:, n * j:n * j + n], q_rows[:, 1 - st.parity, t, :, :], k_diag[:, 1 - st.parity, 0:t + 1, h, :],
                           start=(j == 0), stop=False, skip_group_check=True)
                    diag = ps[:, 0:n * len(heads)].rearrange("p (j n) -> p j n", n=n)[:, :, n - KB:n]
                    mm(diag, mask_s[:, :], eye[:, :].unsqueeze(1).to_broadcast([P, len(heads), KB]),
                       start=False, stop=True, skip_group_check=True).then_inc(filled[st.slot(uses[0])], 1)
                elif what == "probs":
                    if k == 0:
                        pe.wait_ge(m_in_rows, st.upto("P", 2 * 2 * G * 16, 2 * 2 * G * 16))
                    for e in range(k, min(k + 2, len(UNITS))):
                        u, g, n = UNITS[e]
                        wait_for(pe, exp_done, st.upto("P", len(UNITS), e + 1 - ST_BANKS))
                        o = st_tile(st, e)
                        for j in range(n):
                            mm(o[:, j, :], k_diag[:, st.parity, u, :, :], q_rows[:, st.parity, u:BLOCKS, g + j, :],
                               start=(j == 0), stop=False, skip_group_check=True)
                        mm(o[:, :, 0:KB], mask_t[:, :], eye[:, :].unsqueeze(1).to_broadcast([P, n, KB]),
                           start=False, stop=True, skip_group_check=True).then_inc(st_filled, 1)
                elif what == "mix":
                    w = TOKENS - KB * k
                    pe.wait_ge(exp_done, st.upto("P", len(UNITS), UNITS_UPTO[k]))
                    if k == 0:
                        pe.wait_ge(v_done, st.upto("P", 1, 1))
                        wait_for(pe, num_out, st.upto("P", 1, 0))
                    for g in range(G):
                        last = mm(mix[KB * g:KB * g + KB, KB * k:TOKENS], v_diag[:, st.parity, k, :], probs[:, k % PROBS_RING, g, 0:w],
                                  start=(k == 0), stop=(k == BLOCKS - 1), skip_group_check=True)
                    last.then_inc(mix_done, 1)
                elif what == "sums":
                    use = (stage, what, 0, 0)
                    if k == 0:
                        pe.wait_ge(sum_done, st.upto("B", ADDED, ADDED))
                        begin(st, use)
                    ps = bank(st, use)
                    for u in [None] if k == 0 else range(ADDED, BLOCKS):
                        for g in range(G):
                            o, e = ((ps[KB * g:KB * g + KB, :], prob_sum[:, g, :]) if k == 0 else
                                    (ps[KB * g:KB * g + KB, KB * u:TOKENS], probs[:, u % PROBS_RING, g, 0:TOKENS - KB * u]))
                            last = mm(o, par("block"), e, start=(k == 0), stop=(u == BLOCKS - 1), skip_group_check=True)
                    if k == 1:
                        last.then_inc(filled[st.slot(use)], 1)
                elif what == "turn_out":
                    pe.wait_ge(num_out, st.upto("B", 1, 1))
                    turn_tiles(st, uses[0], num_t)
                    turn_tiles(st, uses[1], den_t, after=("B", "sums", 0, 0))
                elif what == "turn":
                    L = ln[k]
                    pe.wait_ge(L["s_xn"], st.upto(stage, 1, 1))
                    turn_tiles(st, uses[0], L["xn"][:, :, :].rearrange("p i d -> p (i d)"))
                elif what == "hidden":
                    L, F = ln["ln1" if stage == "F" else "ln3"], ffn[stage]
                    for j in range(2):
                        ps = begin(st, uses[j], (stage, "turn", "ln1" if stage == "F" else "ln3", 0) if k == j == 0 else None)
                        w = wgu_s[:, HIDDEN * j + P * k:HIDDEN * j + P * k + P]
                        mm(ps, w, L["hi"][:, :], start=True, stop=False)
                        mm(ps, w, L["lo"][:, :], start=False, stop=True).then_inc(filled[st.slot(uses[j])], 1)
                elif what == "down":
                    F = ffn[stage]
                    use, after = (stage, what, 0, 0), None
                    if k in UPS[stage]:
                        pe.wait_ge(F["s_h"], st.upto(stage, len(UPS[stage]), UPS[stage].index(k) + 1))
                    else:
                        after = (stage, "hidden", k, 1)
                    if k == 0:
                        begin(st, use, after)
                    elif after:
                        wait_drained(pe, st, after)
                    for i in range(TILES):
                        last = mm(bank(st, use)[:, P * i:P * i + P], F["h"][:, k, P * i:P * i + P], wd_s[:, P * k:P * k + P],
                                  start=(i == 0 and k == 0), stop=(k == LAST_CHUNK), skip_group_check=True)
                    if k == LAST_CHUNK:
                        last.then_inc(filled[st.slot(use)], 1)
                elif what == "out_proj":
                    L = ln["inner"]
                    ps = begin(st, uses[0], after=("B", "turn", "inner", 0))
                    for i in range(TILES):
                        o, t = ps[:, P * i:P * i + P], slice(P * i, P * i + P)
                        mm(o, L["hi"][:, t], wo_hi[:, :], start=(i == 0), stop=False, skip_group_check=True)
                        mm(o, L["hi"][:, t], wo_lo[:, :], start=False, stop=False, skip_group_check=True)
                        last = mm(o, L["lo"][:, t], wo_hi[:, :], start=False, stop=True, skip_group_check=True)
                    last.then_inc(filled[st.slot(uses[0])], 1)

            run(pe, piece)

        @block.scalar
        def _(act):
            activate = nc.scalar.activation
            act.wait_ge(weights_ready, SETUP)

            def piece(st, stage, what, k):
                uses = work_uses((stage, what, k))
                if what in ("keys", "queries"):
                    if what == "keys":
                        i, scale, bias = 0, 1.0, par("bk")
                        wait_for(act, q_done, st.upto("S", G, 0))
                    else:
                        i, scale, bias = (k + 1) % 2, QSCALE, bq_s[:, k:k + 1]
                        if k == 1:
                            act.wait_ge(k_done, st.upto("S", 1, 1))
                        elif k > 1:
                            act.wait_ge(q_done, st.upto("S", G, k - 1))
                    wait_filled(act, st, uses[0])
                    activate(q_hi[:, i, :], bank(st, uses[0]), ACT.Identity, bias=bias, scale=scale).then_inc(q_high, 1)
                    activate(q_f[:, i, :], bank(st, uses[0]), ACT.Identity, bias=bias, scale=scale
                             ).then_inc(drained[st.slot(uses[0])], 1)
                elif what == "values":
                    wait_filled(act, st, uses[0])
                    activate(v_turned[:, :], bank(st, uses[0]), ACT.Identity, bias=par("bv")).then_inc(drained[st.slot(uses[0])], 1)
                elif what == "probs":
                    for e in range(k, min(k + 2, len(UNITS))):
                        u, g, n = UNITS[e]
                        if g == 0:
                            free_slot(st, u)
                        act.wait_ge(st_filled, st.upto("P", len(UNITS), e + 1))
                        activate(probs[:, u % PROBS_RING, g:g + n, 0:TOKENS - KB * u], st_tile(st, e), ACT.Exp
                                 ).then_inc(exp_done, 1)
                elif what == "norm" and k in NORM_ON_SCALAR:
                    L = ln[k]
                    act.wait_ge(L["s_shift"], st.upto(stage, 1, 1))
                    for i in range(TILES):
                        last = activate(L["xn"][:, i, :], L["src"][:, i, :], ACT.Identity, bias=L["shift"][:, i:i + 1],
                                        scale=L["rstd"][:, i:i + 1])
                    last.then_inc(L["s_xn"], 1)
                elif what == "sums":
                    if k == 0:
                        act.wait_ge(mix_done, st.upto("B", BLOCKS, BLOCKS))
                        nc.scalar.copy(num_t[:, :], mix[:, :]).then_inc(num_out, 1)
                    else:
                        use = (stage, what, 0, 0)
                        wait_filled(act, st, use)
                        nc.scalar.copy(den_t[:, :], bank(st, use)).then_inc(drained[st.slot(use)], 1)
                elif what == "turn":
                    wait_filled(act, st, uses[0])
                    nc.scalar.copy(ln[k]["hi"][:, :], bank(st, uses[0])).then_inc(ln[k]["s_hi"], 1)
                elif what == "hidden":
                    F = ffn[stage]
                    wait_filled(act, st, uses[0])
                    activate(F["th"][:, k % 2, :], bank(st, uses[0]), ACT.Tanh, scale=TANH_SCALE).then_inc(F["s_th"], 1)
                    if (stage, k) in UP_ON_GPSIMD:
                        wait_filled(act, st, uses[1])
                        nc.scalar.copy(F["up"][:, k, :], bank(st, uses[1])).then_inc(drained[st.slot(uses[1])], 1)

            def free_slot(st, u):
                old = u - PROBS_RING
                wait_for(act, mix_done, st.upto("P", BLOCKS, old + 1))
                if old >= 0:
                    act.wait_ge(sum_done, st.upto("P", ADDED, min(max(old + 1, 2), ADDED)))
                elif u == 0:
                    wait_for(act, sum_done, st.upto("P", ADDED, 0))
                if old + BLOCKS == ADDED and "B" in st.stages:
                    wait_filled(act, st, ("B", "sums", 0, 0))

            run(act, piece)

        @block.vector
        def _(dve):
            v = nc.vector
            dve.wait_ge(params_loaded, 16)
            v.tensor_copy(w_hi[:, :], par("wqkv")).then_inc(w_high, 1)
            v.tensor_scalar(wo_g[:, :], par("wo"), par("ln_g"), None, ALU.mult).then_inc(wo_scaled, 1)
            v.tensor_copy(mask_s[:, :], par("mask_s")).then_inc(weights_ready, 1)
            v.tensor_copy(mask_t[:, :], par("mask_t")).then_inc(weights_ready, 1)
            v.tensor_copy(eye[:, :], par("eye")).then_inc(weights_ready, 1)
            v.tensor_scalar(bq_s[:, :], par("bq"), QSCALE, None, ALU.mult).then_inc(weights_ready, 1)
            dve.wait_ge(w_high, 1)
            v.tensor_tensor(w_lo[:, :], par("wqkv"), w_hi[:, :], ALU.subtract).then_inc(weights_ready, 1)
            dve.wait_ge(wo_scaled, 1)
            v.tensor_copy(wo_hi[:, :], wo_g[:, :]).then_inc(w_high, 1)
            dve.wait_ge(w_high, 2)
            v.tensor_tensor(wo_lo[:, :], wo_g[:, :], wo_hi[:, :], ALU.subtract).then_inc(weights_ready, 1)
            dve.wait_ge(bias_product, 1)
            v.tensor_tensor(bo_all[:, :], mix[:, 0:D], par("bo"), ALU.add).then_inc(weights_ready, 1)
            dve.wait_ge(ints_loaded, 32)
            v.tensor_scalar(wgu_s[:, :], wgu_i[:, :], WSCALE, None, ALU.mult).then_inc(weights_ready, 1)
            v.tensor_scalar(wd_s[:, :], wd_i[:, :], WSCALE, None, ALU.mult).then_inc(weights_ready, 1)
            dve.wait_ge(weights_ready, SETUP)
            dve.wait_ge(k_cleared, 1)

            def piece(st, stage, what, k):
                uses = work_uses((stage, what, k))
                if what in ("keys", "queries"):
                    wait_drained(dve, st, uses[0])
                    i = 0 if what == "keys" else (k + 1) % 2
                    o, low, s = ((k_rows[:, :].rearrange("p (u c) -> p u c", c=KB), par("low_k"), k_done)
                                 if what == "keys" else (q_rows[:, 1 - st.parity, :, k, :], par("low_q"), q_done))
                    v.scalar_tensor_tensor(out=o, in0=q_hi[:, i, :].rearrange("p (u c) -> p u c", c=KB), scalar=low,
                                           in1=q_f[:, i, :].rearrange("p (u c) -> p u c", c=KB),
                                           op0=ALU.mult, op1=ALU.add).then_inc(s, 1)
                if what == "keys":
                    dve.wait_ge(k_done, st.upto("S", 1, 1))
                    for h in range(H):
                        r = slice(KB * h, KB * h + KB)
                        last = v.tensor_copy(k_diag[r, 1 - st.parity, :, h, :], k_rows[r, :].rearrange("p (u c) -> p u c", c=KB))
                    last.then_inc(k_placed, 1)
                elif what == "values":
                    wait_drained(dve, st, uses[0])
                    v.transpose(v_diag[:, 1 - st.parity, :, :].rearrange("p u c -> p (u c)"), v_turned[:, :]).then_inc(v_done, 1)
                elif what == "scores":
                    t, heads = SCORE_TILES[k]
                    n, nh = KB * (t + 1), len(heads)
                    wait_filled(dve, st, uses[0])
                    v.tensor_reduce(m_all[:, t // 8, heads[0]:heads[0] + nh, t % 8],
                                    bank(st, uses[0])[:, 0:n * nh].rearrange("p (j n) -> p j n", n=n), AX.X, ALU.max
                                    ).then_inc(drained[st.slot(uses[0])], 1)
                elif what == "maxima":
                    last_tile = (FIRST_HALF if k == 0 else len(SCORE_TILES)) - 1
                    wait_drained(dve, st, ("S", "scores", last_tile, 0))
                    m = m_all[:, k, :, :].rearrange("p h t -> p (h t)")
                    v.tensor_copy(m_parts[:, k, 0, :], m).then_inc(m_high, 1)
                    dve.wait_ge(m_high, st.upto("S", 2, k + 1))
                    v.tensor_tensor(m_parts[:, k, 1, :], m, m_parts[:, k, 0, :], ALU.subtract).then_inc(m_split, 1)
                    dve.wait_ge(m_split, st.upto("S", 2, k + 1))
                    wait_for(dve, m_in_rows, st.upto("S", 4 * G * 16, 0))
                    v.transpose(m_turned[:, k, :, :].rearrange("p a c -> p (a c)"),
                                m_parts[:, k, :, :].rearrange("p a c -> p (a c)")).then_inc(m_turn, 1)
                elif what == "turn_out":
                    wait_filled(dve, st, uses[1])
                    v.reciprocal(rden[:, :], bank(st, uses[1]).rearrange("p (c d) -> p c d", d=HD)[:, :, 0]
                                 ).then_inc(drained[st.slot(uses[1])], 1)
                    wait_drained(dve, st, uses[1])
                    v.tensor_tensor(attended[:, :, :].rearrange("p i (c d) -> p (i c) d", d=HD),
                                    bank(st, uses[0]).rearrange("p (c d) -> p c d", d=HD),
                                    rden[:, :].unsqueeze(2).to_broadcast([P, TILES * G * H, HD]), ALU.mult
                                    ).then_inc(drained[st.slot(uses[0])], 1)
                elif what == "stats":
                    L = ln[k]
                    if k == "ln1":
                        dve.wait_ge(x_loaded, st.upto("F", 16, 16))
                    else:
                        wait_drained(dve, st, {"ln2": ("F", "down", 0, 0), "inner": ("B", "turn_out", 0, 0),
                                               "ln3": ("B", "out_proj", 0, 0)}[k])
                    for i in range(TILES):
                        v.bn_stats(L["bn"][:, i, :], L["src"][:, i, :]).then_inc(L["s_bn"], 1)
                    dve.wait_ge(L["s_bn"], st.upto(stage, TILES, TILES))
                    v.memset(gate[:, :], 0.0)
                    for i in range(TILES):
                        v.bn_aggr(L["mv"][:, i, :], L["bn"][:, i, :]).then_inc(L["s_mv"], 1)
                elif what == "norm" and k not in NORM_ON_SCALAR:
                    L = ln[k]
                    dve.wait_ge(L["s_rstd"], st.upto(stage, 1, 1))
                    for i in range(TILES):
                        last = v.tensor_scalar(L["xn"][:, i, :], L["src"][:, i, :], L["mv"][:, i, 0:1], L["rstd"][:, i:i + 1],
                                               ALU.subtract, ALU.mult)
                    last.then_inc(L["s_xn"], 1)
                elif what == "turn":
                    L = ln[k]
                    dve.wait_ge(L["s_hi"], st.upto(stage, 1, 1))
                    v.tensor_tensor(L["lo"][:, :], bank(st, uses[0]), L["hi"][:, :], ALU.subtract
                                    ).then_inc(drained[st.slot(uses[0])], 1)
                elif what == "gated":
                    uses = work_uses((stage, "hidden", k))
                    F = ffn[stage]
                    dve.wait_ge(F["s_th"], st.upto(stage, CHUNKS, k + 1))
                    v.scalar_tensor_tensor(out=F["h"][:, k, :], in0=F["th"][:, k % 2, :], scalar=1.0, in1=bank(st, uses[0]),
                                           op0=ALU.add, op1=ALU.mult).then_inc(drained[st.slot(uses[0])], 1)
                    if (stage, k) not in UP_ON_GPSIMD:
                        wait_filled(dve, st, uses[1])
                        wait_drained(dve, st, uses[0])
                        v.tensor_tensor(F["h"][:, k, :], F["h"][:, k, :], bank(st, uses[1]), ALU.mult
                                        ).then_inc(drained[st.slot(uses[1])], 1)
                elif what == "down" and k == LAST_CHUNK:
                    uses = [(stage, what, 0, 0)]
                    wait_filled(dve, st, uses[0])
                    if stage == "B":
                        dve.wait_ge(y_free, 16 + st.upto("B", 16, 0))
                    else:
                        wait_for(dve, x_mid_done, st.upto("F", 1, 0))
                    o, res = (x_front, x_in) if stage == "F" else (y, x_att)
                    v.scalar_tensor_tensor(out=flat(o), in0=bank(st, uses[0]), scalar=FFN_SCALE, in1=flat(res),
                                           op0=ALU.mult, op1=ALU.add).then_inc(drained[st.slot(uses[0])], 1)
                elif what == "out_proj":
                    wait_filled(dve, st, uses[0])
                    dve.wait_ge(x_mid_done, st.upto("B", 1, 1))
                    v.tensor_tensor(x_att[:, :, :], bank(st, uses[0]).rearrange("p (i d) -> p i d", d=D), entry(x_mid, st.b - 1),
                                    ALU.add).then_inc(drained[st.slot(uses[0])], 1)

            def flat(t):
                return t[:, :, :].rearrange("p i d -> p (i d)")

            run(dve, piece)

        @block.gpsimd
        def _(pool):
            g_ = nc.gpsimd
            g_.memset(k_diag[:, :, :, :, :], 0.0).then_inc(k_cleared, 1)
            g_.memset(y[:, 0, 0:1], 0.0).then_inc(y_free, 16)
            pool.wait_ge(weights_ready, SETUP)

            def piece(st, stage, what, k):
                uses = work_uses((stage, what, k))
                if what == "add":
                    w = TOKENS - KB * k
                    pool.wait_ge(exp_done, st.upto("P", len(UNITS), UNITS_UPTO[k]))
                    e = probs[:, k % PROBS_RING, :, 0:w]
                    if k == 0:
                        if "B" in st.stages:
                            wait_filled(pool, st, ("B", "sums", 0, 0))
                        g_.tensor_tensor(prob_sum[:, :, 0:KB], e[:, :, 0:KB],
                                         par("zero").unsqueeze(2).to_broadcast([P, G, KB]), ALU.add).then_inc(sum_done, 1)
                    elif k == 1:
                        g_.tensor_tensor(prob_sum[:, :, KB:TOKENS], probs[:, 0, :, KB:TOKENS], e, ALU.add).then_inc(sum_done, 1)
                    else:
                        pool.wait_ge(sum_done, st.upto("P", ADDED, k))
                        o = prob_sum[:, :, KB * k:TOKENS]
                        g_.tensor_tensor(o, o, e, ALU.add).then_inc(sum_done, 1)
                elif what == "stats":
                    L = ln[k]
                    pool.wait_ge(L["s_mv"], st.upto(stage, TILES, TILES))
                    g_.tensor_tensor(L["var"][:, :], L["mv"][:, :, 1], par("eps"), ALU.add).then_inc(L["s_var"], 1)
                    pool.wait_ge(L["s_var"], st.upto(stage, 1, 1))
                    g_.tensor_tensor(L["rstd"][:, :], L["var"][:, :], par("neg_half"), ALU.pow).then_inc(L["s_rstd"], 1)
                    if k in NORM_ON_SCALAR:
                        pool.wait_ge(L["s_rstd"], st.upto(stage, 1, 1))
                        g_.tensor_tensor(L["minus"][:, :], L["rstd"][:, :], par("minus_one"), ALU.mult).then_inc(L["s_minus"], 1)
                        pool.wait_ge(L["s_minus"], st.upto(stage, 1, 1))
                        g_.tensor_tensor(L["shift"][:, :], L["mv"][:, :, 0], L["minus"][:, :], ALU.mult).then_inc(L["s_shift"], 1)
                elif what == "gated" and (stage, k) in UP_ON_GPSIMD:
                    F = ffn[stage]
                    for j in range(2):
                        wait_drained(pool, st, (stage, "hidden", k, j))
                    g_.tensor_tensor(F["h"][:, k, :], F["h"][:, k, :], F["up"][:, k, :], ALU.mult
                                     ).then_inc(F["s_h"], 1)
                elif what == "carry":
                    wait_drained(pool, st, ("F", "down", 0, 0))
                    g_.tensor_tensor(entry(x_mid, st.b + 2), x_front[:, :, :],
                                     bo_all[:, :].unsqueeze(1).to_broadcast([P, TILES, D]), ALU.add).then_inc(x_mid_done, 1)

            run(pool, piece)

    return nc


def layout(inputs):
    f = {n[len("L0_attn_"):]: np.asarray(a) for n, a in inputs.items() if n.startswith("L0_attn_")}
    one = np.float32

    def rows(w, keep):
        o = np.zeros(w.shape[:-2] + (H, 4, HD), one)
        for slot in range(3):
            o[..., slot, :] = w
        return o.reshape(keep + (-1,))

    wq, wk = rows(f["Wq"].reshape(D, G, H, HD), (D,)), rows(f["Wk"].reshape(D, H, HD), (D,))
    bq = rows(f["bq"].reshape(G, H, HD), (G,)).T
    wv, bv = np.zeros((D, H, H, HD), one), np.zeros((H, H, HD), one)
    for h in range(H):
        wv[:, h, h], bv[h, h] = f["Wv"][:, HD * h:HD * h + HD], f["bv"][HD * h:HD * h + HD]
    bk = rows(f["bk"].reshape(H, HD), ())
    bk = bk.reshape(H, 4, HD)
    bk[:, 3, 0:2] = -1.0
    row = np.arange(P)
    slot = (row // HD) % 4
    a, k = np.arange(P)[:, None], np.arange(P)[None, :] % KB
    cols = {
        "wqkv": np.concatenate([wq, wk, wv.reshape(D, P)], 1), "wo": f["Wo"], "ln_b": np.repeat(f["ln_b"][:, None], P, 1),
        "bo": np.repeat(f["bo"][None], P, 0), "bv": bv.reshape(P, 1), "bq": bq, "bk": bk.reshape(P, 1),
        "ln_g": f["ln_g"][:, None], "ident": np.eye(P, dtype=one),
        "mask_s": np.where((a < KB) & (a > k), one(MASKED), one(0)),
        "mask_t": np.where((a < KB) & (a < k), one(MASKED), one(0)),
        "eye": np.eye(P, KB, dtype=one), "block": (row[:, None] // KB == np.arange(H * HD)[None] // HD).astype(one),
        "low_q": np.where(slot == 2, one(-1), one(0))[:, None], "low_k": np.where(slot == 1, one(-1), one(0))[:, None],
        "neg_half": np.full((P, TILES), -0.5, one), "eps": np.full((P, TILES), EPS, one),
        "minus_one": np.full((P, TILES), -1, one), "zero": np.zeros((P, 1), one),
    }
    packed = np.empty((P, PACKED), one)
    for name, (lo, hi) in PACK.items():
        packed[:, lo:hi] = cols[name]
    wg, wu, wd = (np.asarray(inputs["L0_ffn_" + n]) for n in ("w_gate", "w_up", "w_down"))
    wgu = np.ascontiguousarray(np.concatenate([wg, wu], 0).T)
    wd = np.ascontiguousarray(wd.T.reshape(CHUNKS, P, D).transpose(1, 0, 2).reshape(P, HIDDEN))
    return np.ascontiguousarray(f["x"]), packed, wgu, wd


def kernel(**inputs):
    import concourse.bacc as bacc
    from concourse.bass_utils import run_bass_kernel_spmd

    nc = bacc.Bacc("TRN2", target_bir_lowering=False, num_devices=1)
    arrays, args = {}, []
    for name, a in zip(("x", "packed", "wgu", "wd"), layout(inputs)):
        arrays[name] = a
        args.append(nc.dram_tensor(name, a.shape, mybir.dt.from_np(a.dtype), kind="ExternalInput").ap())
    out = nc.dram_tensor("out", (ENTRIES, TOKENS, D), F32, kind="ExternalOutput").ap()
    macaron(nc, *args, out)
    r = run_bass_kernel_spmd(nc, [arrays], core_ids=[0])
    return r.results[0]["out"]
```

```python
from contextlib import ExitStack

import numpy as np

import concourse.bass as bass
from concourse import mybir

F32 = mybir.dt.float32
F16 = mybir.dt.float16
BF16 = mybir.dt.bfloat16
I32 = mybir.dt.int32
ALU = mybir.AluOpType
ACT = mybir.ActivationFunctionType
AX = mybir.AxisListType

P = 128
ENTRIES, TOKENS, D = 8, 512, 128
TILES = TOKENS // P
G, H, HD = 4, 4, 8
KB = 32
BLOCKS = TOKENS // KB
CHUNKS = 3
HIDDEN = CHUNKS * P
LAST_CHUNK = CHUNKS - 1
EPS = 1e-5
WSCALE = 2.0 ** -7
QSCALE = float(HD) ** -0.5
TANH_SCALE = 0.5 * 128.0 / 127.0
FFN_SCALE = 0.25 * (128.0 / 127.0) ** 3
MASKED = -1e30
PROBS_RING = 8
ADDED = 11

PACK = {}
_at = 0
for _name, _n in (("ident", P), ("neg_half", TILES), ("eps", TILES), ("minus_one", TILES), ("zero", 1),
                  ("wqkv", G * P + 2 * P), ("wo", D), ("ln_b", P), ("bo", D), ("bq", G), ("bk", 1), ("bv", 1), ("ln_g", 1),
                  ("mask_s", P), ("mask_t", P), ("eye", KB), ("block", H * HD), ("low_q", 1), ("low_k", 1)):
    PACK[_name] = (_at, _at + _n)
    _at += _n
PACKED = _at
FIRST_PACKED = PACK["wqkv"][0]


SCORE_TILES = [(t, tuple(range(h, h + n))) for t in range(BLOCKS)
               for n in ((4 if t < 4 else 2 if t < 8 else 1),) for h in range(0, H, n)]
FIRST_HALF = sum(t < BLOCKS // 2 for t, _ in SCORE_TILES)

SCORE_BANKS, OTHER_BANKS = 2, 3
ST_BANKS = 2
WORK = SCORE_BANKS + OTHER_BANKS
UNITS = [(u, g, n) for u in range(BLOCKS) for n in (1 if TOKENS - KB * u > 256 else 2 if TOKENS - KB * u > 128 else 4,)
         for g in range(0, G, n)]
assert len(UNITS) % ST_BANKS == 0
UNITS_UPTO = [sum(1 for v, _, _ in UNITS if v <= u) for u in range(BLOCKS)]


ORDERS = {
    "F": """
        F.stats.ln1 F.norm.ln1 F.turn.ln1 F.weights.0 F.hidden.0 F.gated.0 F.hidden.1 F.gated.1 F.weights.1 F.weights.2
        F.hidden.2 F.gated.2 F.down.0 F.down.1 F.down.2 F.stats.ln2 F.norm.ln2 F.carry.0 F.turn.ln2
    """,
    "FS": """
        F.stats.ln1 S.keys.0 S.queries.0 S.queries.1 S.queries.2 S.queries.3 S.scores.0 S.scores.1 F.norm.ln1 F.turn.ln1
        S.scores.2 S.scores.3 S.values.0 S.scores.4 F.hidden.0 S.scores.5 S.scores.6 F.gated.0 S.scores.7 S.scores.8
        F.hidden.1 S.scores.9 S.scores.10 F.gated.1 S.scores.11 F.hidden.2 S.scores.12 S.scores.13 S.scores.14
        S.scores.15 S.scores.16 S.scores.17 S.scores.18 F.gated.2 F.down.0 F.down.1 S.scores.19 S.scores.20 S.scores.21
        S.scores.22 S.scores.23 S.scores.24 S.scores.25 S.scores.26 S.maxima.0 S.scores.27 S.scores.28 F.down.2
        S.scores.29 F.carry.0 S.scores.30 S.scores.31 S.scores.32 S.scores.33 F.stats.ln2 S.scores.34 S.scores.35
        S.scores.36 S.scores.37 S.scores.38 S.scores.39 S.scores.40 S.scores.41 S.scores.42 S.scores.43 F.norm.ln2
        S.maxima.1 F.turn.ln2
    """,
    "FSP": """
        F.stats.ln1 S.keys.0 S.queries.0 S.queries.1 S.queries.2 S.queries.3 S.values.0 P.probs.0 S.scores.0 S.scores.1
        P.probs.2 S.scores.2 S.scores.3 P.probs.4 P.probs.6 S.scores.4 S.scores.5 P.mix.0 S.scores.6 S.scores.7
        F.norm.ln1 P.add.0 P.probs.8 S.scores.8 F.turn.ln1 P.probs.10 P.add.1 S.scores.9 S.scores.10 P.probs.12
        S.scores.11 P.probs.14 S.scores.12 F.hidden.0 P.add.2 P.add.3 S.maxima.0 S.scores.13 F.gated.0 S.scores.14
        P.probs.16 P.probs.18 S.scores.15 S.scores.16 P.probs.20 P.mix.1 P.probs.22 S.scores.17 F.hidden.1 F.gated.1
        S.scores.18 S.scores.19 P.probs.24 P.mix.2 P.probs.26 F.hidden.2 P.add.4 F.gated.2 S.scores.20 S.scores.21
        P.probs.28 P.add.5 P.add.6 F.down.0 P.probs.30 F.down.1 S.scores.22 S.scores.23 F.down.2 P.probs.32 S.scores.24
        S.scores.25 P.mix.3 S.scores.26 F.stats.ln2 P.probs.34 P.mix.4 S.scores.27 S.scores.28 F.carry.0 P.probs.36
        P.mix.5 S.scores.29 P.mix.6 S.scores.30 S.scores.31 P.mix.7 S.scores.32 S.scores.33 F.norm.ln2 P.probs.38
        S.scores.34 P.mix.8 S.scores.35 S.scores.36 P.mix.9 P.add.7 P.add.8 S.scores.37 S.scores.38 P.mix.10 S.scores.39
        P.probs.40 S.scores.40 S.scores.41 P.add.9 F.turn.ln2 P.add.10 P.mix.11 S.scores.42 S.scores.43 P.probs.42
        P.mix.12 P.mix.13 P.mix.14 P.mix.15 S.maxima.1
    """,
    "FSPB": """
        S.keys.0 S.queries.0 S.queries.1 S.queries.2 S.values.0 B.sums.0 F.stats.ln1 B.sums.1 S.queries.3 B.turn_out.0
        P.probs.0 P.probs.2 S.scores.0 S.scores.1 B.stats.inner P.probs.4 S.scores.2 S.scores.3 P.probs.6 P.mix.0
        F.norm.ln1 S.scores.4 P.probs.8 S.scores.5 P.add.0 B.norm.inner S.scores.6 P.mix.1 S.scores.7 S.scores.8
        P.probs.10 S.scores.9 S.scores.10 B.turn.inner S.scores.11 P.probs.12 S.scores.12 F.turn.ln1 P.mix.2 P.probs.14
        P.add.1 S.scores.13 S.scores.14 P.add.2 B.out_proj.0 P.probs.16 S.scores.15 S.scores.16 F.hidden.0 F.gated.0
        P.probs.18 P.mix.3 B.stats.ln3 S.scores.17 F.hidden.1 S.scores.18 F.gated.1 P.probs.20 P.mix.4 S.scores.19
        S.scores.20 P.add.3 P.add.4 F.hidden.2 F.gated.2 P.probs.22 F.down.0 P.probs.24 S.scores.21 S.scores.22 F.down.1
        S.scores.23 B.norm.ln3 P.probs.26 P.add.5 S.scores.24 F.down.2 S.scores.25 S.scores.26 B.turn.ln3 P.probs.28
        P.mix.5 S.scores.27 S.scores.28 P.probs.30 P.mix.6 F.stats.ln2 S.scores.29 P.probs.32 S.scores.30 B.hidden.0
        P.add.6 B.gated.0 P.probs.34 S.scores.31 P.mix.7 S.scores.32 S.maxima.0 B.hidden.1 S.scores.33 P.probs.36
        S.scores.34 F.norm.ln2 P.mix.8 P.mix.9 P.probs.38 B.gated.1 S.scores.35 S.scores.36 B.hidden.2 P.probs.40
        S.scores.37 P.mix.10 P.add.7 P.add.8 P.add.9 S.scores.38 P.mix.11 S.scores.39 B.gated.2 B.down.0 P.mix.12
        P.mix.13 S.scores.40 S.scores.41 P.add.10 P.probs.42 F.turn.ln2 B.down.1 S.scores.42 S.scores.43 S.maxima.1
        P.mix.14 P.mix.15 B.down.2 F.carry.0
    """,
    "SPB": """
        S.keys.0 S.values.0 S.queries.0 S.queries.1 S.queries.2 S.queries.3 B.sums.0 B.sums.1 P.probs.0 S.scores.0
        S.scores.1 B.turn_out.0 S.scores.2 P.probs.2 S.scores.3 P.probs.4 S.scores.4 B.stats.inner P.add.0 P.probs.6
        S.scores.5 S.scores.6 P.probs.8 P.mix.0 P.probs.10 P.probs.12 S.scores.7 S.scores.8 S.scores.9 P.probs.14
        S.scores.10 P.probs.16 S.scores.11 S.scores.12 P.add.1 P.add.2 P.mix.1 S.scores.13 S.scores.14 B.norm.inner
        S.scores.15 S.scores.16 B.turn.inner S.scores.17 P.probs.18 S.scores.18 P.probs.20 B.out_proj.0 P.add.3
        P.probs.22 S.scores.19 S.scores.20 P.probs.24 P.mix.2 B.stats.ln3 P.probs.26 P.mix.3 S.scores.21 S.scores.22
        P.mix.4 P.probs.28 B.norm.ln3 S.scores.23 S.scores.24 S.scores.25 P.probs.30 S.scores.26 P.add.4 S.scores.27
        S.scores.28 S.scores.29 B.turn.ln3 S.scores.30 P.add.5 P.add.6 S.maxima.0 P.probs.32 S.scores.31 P.mix.5 P.mix.6
        P.probs.34 S.scores.32 B.hidden.0 B.gated.0 S.scores.33 S.scores.34 P.probs.36 B.hidden.1 B.gated.1 S.scores.35
        S.scores.36 P.mix.7 P.mix.8 P.mix.9 P.add.7 S.scores.37 B.down.0 S.scores.38 B.hidden.2 P.mix.10 S.scores.39
        S.scores.40 S.scores.41 S.scores.42 P.add.8 S.scores.43 P.probs.38 P.probs.40 B.down.1 P.add.9 P.add.10
        P.probs.42 P.mix.11 P.mix.12 S.maxima.1 B.gated.2 P.mix.13 P.mix.14 B.down.2 P.mix.15
    """,
    "PB": """
        B.sums.0 B.sums.1 B.turn_out.0 B.stats.inner B.norm.inner P.probs.0 P.probs.2 P.probs.4 P.probs.6 P.probs.8
        P.probs.10 P.add.0 P.add.1 B.turn.inner P.probs.12 P.probs.14 P.add.2 B.out_proj.0 P.probs.16 P.mix.0 P.probs.18
        P.mix.1 P.probs.20 P.probs.22 P.mix.2 P.probs.24 B.stats.ln3 P.mix.3 P.probs.26 P.mix.4 P.add.3 B.norm.ln3
        P.add.4 P.probs.28 B.turn.ln3 P.probs.30 P.mix.5 P.probs.32 P.add.5 B.hidden.0 B.gated.0 P.mix.6 P.probs.34
        B.hidden.1 P.mix.7 P.add.6 P.probs.36 P.add.7 P.mix.8 P.probs.38 P.mix.9 B.gated.1 B.down.0 P.add.8 B.hidden.2
        B.gated.2 P.probs.40 P.add.9 P.add.10 B.down.1 P.mix.10 P.mix.11 B.down.2 P.probs.42 P.mix.12 P.mix.13 P.mix.14
        P.mix.15
    """,
    "B": """
        B.sums.0 B.sums.1 B.turn_out.0 B.stats.inner B.norm.inner B.turn.inner B.out_proj.0 B.stats.ln3 B.norm.ln3
        B.turn.ln3 B.hidden.0 B.gated.0 B.hidden.1 B.gated.1 B.hidden.2 B.down.0 B.down.1 B.gated.2 B.down.2
    """,
}


def pieces(kind):
    split = (word.split(".") for word in ORDERS[kind].split())
    return [(stage, what, int(k) if k.isdigit() else k) for stage, what, k in split]


def work_uses(item):
    stage, what, k = item
    n = {"keys": 1, "queries": 1, "values": 1, "scores": 1, "sums": 1, "turn_out": 2, "turn": 1,
         "hidden": 2, "down": 1, "out_proj": 1}.get(what, 0)
    if what in ("sums", "down") and k > 0:
        n = 0
    return [(stage, what, k, j) for j in range(n)]


UP_ON_GPSIMD = (("F", 0), ("B", 0))
UPS = {stage: [k for s, k in UP_ON_GPSIMD if s == stage] for stage in "FB"}
STAGES = "FSPB"
ADD_ON_VECTOR = ("PB",)
NORM_ON_VECTOR = ("F", "PB", "B")


class Plan:

    def __init__(self, order):
        self.items = order
        uses = [u for item in order for u in work_uses(item)]
        scores = [u for u in uses if u[1] == "scores"]
        others = [u for u in uses if u[1] != "scores"]
        shift = others.index(LN2_TURN) if LN2_TURN in others else 0
        self.slot = {u: i % SCORE_BANKS for i, u in enumerate(scores)}
        self.slot.update({u: SCORE_BANKS + (i - shift) % OTHER_BANKS for i, u in enumerate(others)})
        self.fills, self.rank = [0] * WORK, {}
        for u in uses:
            self.fills[self.slot[u]] += 1
            self.rank[u] = self.fills[self.slot[u]]


LN2_TURN = ("F", "turn", "ln2", 0)
PLANS = {kind: Plan(pieces(kind)) for kind in ORDERS}


class Step:

    LEAD = {"F": 2, "S": 1, "P": 0, "B": -1}

    def __init__(self, b, parity):
        self.b, self.parity = b, parity
        self.before = {stage: b + lead for stage, lead in self.LEAD.items()}
        self.stages = STAGES
        if isinstance(b, int):
            self.stages = self.kind(b)
            self.before = {stage: min(max(n, 0), ENTRIES) for stage, n in self.before.items()}

        self.plan = PLANS[self.stages]

    def kind(self, b):
        return "".join(stage for stage in STAGES if 0 <= b + self.LEAD[stage] < ENTRIES)

    def upto(self, stage, per, k):
        return self.before[stage] * per + k

    def slot(self, use):
        return self.plan.slot[use]

    def work(self, use):
        return self.work_before(self.slot(use)) + self.plan.rank[use]

    def work_before(self, slot):
        if isinstance(self.b, int):
            return sum(PLANS[self.kind(b)].fills[slot] for b in range(-2, self.b))
        full = PLANS[STAGES].fills[slot]
        return self.b * full + (sum(PLANS[self.kind(b)].fills[slot] for b in range(-2, 1)) - full)


def wait_for(eng, sem, value):
    if not isinstance(value, int) or value > 0:
        eng.wait_ge(sem, value)


def macaron(nc, x, packed, wgu, wd, out):
    x_v = x.rearrange("e (i p) d -> e p i d", p=P)
    out_v = out.rearrange("e (i p) d -> e p i d", p=P)
    with ExitStack() as ctx:
        def sb(name, shape, dt=F32):
            return ctx.enter_context(nc.sbuf_tensor(name, [P] + shape, dt))

        def sem(name):
            return ctx.enter_context(nc.semaphore(name))

        params = sb("params", [PACKED])

        def par(name):
            a, z = PACK[name]
            return params[:, a:z]

        wgu_i = sb("wgu_i", [2 * HIDDEN], I32)
        wd_i = sb("wd_i", [HIDDEN], I32)
        wgu_s = sb("wgu_s", [2 * HIDDEN], F16)
        wd_s = sb("wd_s", [HIDDEN])
        NQKV = G * P + 2 * P
        w_hi = sb("w_hi", [NQKV], F16)
        w_lo = sb("w_lo", [NQKV], F16)
        wo_g = sb("wo_g", [D])
        wo_hi = sb("wo_hi", [D], F16)
        wo_lo = sb("wo_lo", [D], F16)
        bo_all = sb("bo_all", [D])
        bq_s = sb("bq_s", [G])
        mask_s = sb("mask_s_b", [P], BF16)
        mask_t = sb("mask_t_b", [P], BF16)
        eye = sb("eye_b", [KB], BF16)
        ident = par("ident")
        WK, WV = G * P, G * P + P

        x_in = sb("x_in", [TILES, D])
        x_front = sb("x_front", [TILES, D])
        x_mid = sb("x_mid", [ENTRIES, TILES, D])
        x_att = sb("x_att", [TILES, D])
        y = sb("y", [TILES, D])
        ln = {}
        for name in ("ln1", "ln2", "inner", "ln3"):
            ln[name] = dict(
                bn=sb(f"{name}_bn", [TILES, 6]), mv=sb(f"{name}_mv", [TILES, 2]), rstd=sb(f"{name}_rstd", [TILES]),
                var=sb(f"{name}_var", [TILES]), s_var=sem(f"{name}_var_eps"),
                minus=sb(f"{name}_minus_rstd", [TILES]), s_minus=sem(f"{name}_minus_rstd_ready"),
                shift=sb(f"{name}_shift", [TILES]), s_shift=sem(f"{name}_shift_ready"),
                xn=sb(f"{name}_xn", [TILES, D]), hi=sb(f"{name}_hi", [TOKENS], F16), lo=sb(f"{name}_lo", [TOKENS], F16),
                s_bn=sem(f"{name}_tile_stats"), s_mv=sem(f"{name}_moments"), s_rstd=sem(f"{name}_rstd_ready"),
                s_xn=sem(f"{name}_normalised"), s_hi=sem(f"{name}_high_part"))
        waits_here = sb("waits_here", [1])
        attended = sb("attended", [TILES, D])
        ln["ln1"]["src"], ln["ln2"]["src"], ln["inner"]["src"], ln["ln3"]["src"] = x_in, x_front, attended, x_att
        ffn = {}
        for st in "FB":
            ffn[st] = dict(
                th=sb(f"{st}_th", [2, TOKENS]), h=sb(f"{st}_h", [CHUNKS, TOKENS]),
                up=sb(f"{st}_up", [CHUNKS, TOKENS]), s_h=sem(f"{st}_hidden_ready"),
                s_th=sem(f"{st}_tanh_ready"))
        q_hi = sb("q_hi", [2, TOKENS], F16)
        q_f = sb("q_f", [2, TOKENS])
        q_rows = sb("q_rows", [2, BLOCKS, G, KB], F16)
        k_rows = sb("k_rows", [TOKENS], F16)
        k_diag = sb("k_diag", [2, BLOCKS, H, KB], F16)
        v_turned = sb("v_turned", [TOKENS])
        v_diag = sb("v_diag", [2, BLOCKS, H * HD])
        m_all = sb("m_all", [2, H, 8])
        m_parts = sb("m_parts", [2, 2, KB], F16)
        m_turned = sb("m_turned", [2, 2, KB], F16)
        probs = sb("probs", [PROBS_RING, G, TOKENS])
        prob_sum = sb("prob_sum", [G, TOKENS])
        num_t = sb("num_t", [TOKENS])
        den_t = sb("den_t", [TOKENS])
        rden = sb("rden", [TILES * G * H])

        work = ctx.enter_context(nc.psum_tensor("work", [P, WORK, 512], F32))
        mix = ctx.enter_context(nc.psum_tensor("mix", [P, 512], F32))
        st_ps = ctx.enter_context(nc.psum_tensor("st_ps", [P, ST_BANKS, 512], F32))

        def bank(st, use):
            return work[:, st.slot(use), :]

        first_loaded, params_loaded, ints_loaded = sem("first_loaded"), sem("params_loaded"), sem("ints_loaded")
        ffn_ready, x_loaded, y_free = sem("ffn_weights_ready"), sem("x_loaded"), sem("y_free")
        weights_ready, wo_scaled, w_high, bias_product = sem("weights_ready"), sem("wo_scaled"), sem("w_high"), sem("bias_product")
        k_cleared = sem("k_diag_cleared")
        filled = [sem(f"work{s}_filled") for s in range(WORK)]
        drained = [sem(f"work{s}_drained") for s in range(WORK)]
        q_high, q_done, k_done, k_placed = sem("q_high"), sem("q_rows_ready"), sem("k_rows_ready"), sem("k_diag_ready")
        v_done = sem("v_diag_ready")
        m_high, m_split, m_turn, m_in_rows = sem("m_high"), sem("m_split"), sem("m_turned_ready"), sem("m_in_q_rows")
        st_filled, exp_done, mix_done, sum_done = sem("st_filled"), sem("exp_done"), sem("mix_done"), sem("prob_sum_done")
        num_out = sem("num_out")
        x_mid_done = sem("x_mid_done")
        SETUP = 7

        block = ctx.enter_context(nc.Block())

        def run(eng, piece):
            step(eng, piece, Step(-2, 0))
            if eng is not nc.sync:
                eng.wait_ge(weights_ready, SETUP)
                eng.wait_ge(k_cleared, 1)
            for b in range(-1, 1):
                step(eng, piece, Step(b, b % 2))
            with eng.Fori(1, 4, 2) as b:
                step(eng, piece, Step(b, 1))
                step(eng, piece, Step(b + 1, 0))
            for b in range(5, ENTRIES + 1):
                step(eng, piece, Step(b, b % 2))

        def step(eng, piece, st):
            for item in st.plan.items:
                piece(st, *item)

        def wait_drained(eng, st, use):
            eng.wait_ge(drained[st.slot(use)], st.work(use))

        def wait_filled(eng, st, use):
            eng.wait_ge(filled[st.slot(use)], st.work(use))

        def add(eng, st, k):
            e = probs[:, k % PROBS_RING, :, 0:TOKENS - KB * k]
            eng.wait_ge(exp_done, st.upto("P", len(UNITS), UNITS_UPTO[k]))
            if k == 0:
                if "B" in st.stages:
                    wait_filled(eng, st, ("B", "sums", 0, 0))
                eng.tensor_tensor(prob_sum[:, :, 0:KB], e[:, :, 0:KB],
                                  par("zero").unsqueeze(2).to_broadcast([P, G, KB]), ALU.add).then_inc(sum_done, 1)
            elif k == 1:
                eng.tensor_tensor(prob_sum[:, :, KB:TOKENS], probs[:, 0, :, KB:TOKENS], e, ALU.add).then_inc(sum_done, 1)
            else:
                eng.wait_ge(sum_done, st.upto("P", ADDED, k))
                o = prob_sum[:, :, KB * k:TOKENS]
                eng.tensor_tensor(o, o, e, ALU.add).then_inc(sum_done, 1)

        def entry(t, e):
            return t[:, e] if isinstance(e, int) else t[:, bass.ds(e, 1)].rearrange("p e i d -> p (e i) d")

        @block.sync
        def _(sp):
            sp.dma_start(x_in[:, :, :], x_v[0]).then_inc(x_loaded, 16)
            sp.dma_start(params[:, 0:FIRST_PACKED], packed[:, 0:FIRST_PACKED]).then_inc(first_loaded, 16)
            sp.dma_start(wgu_i[:, :], wgu).then_inc(ints_loaded, 16)
            sp.dma_start(wd_i[:, :], wd).then_inc(ints_loaded, 16)
            sp.dma_start(params[:, FIRST_PACKED:PACKED], packed[:, FIRST_PACKED:PACKED]).then_inc(params_loaded, 16)

            def piece(st, stage, what, k):
                if (stage, what, k) == ("F", "down", LAST_CHUNK) and (not isinstance(st.b, int) or st.b + 3 < ENTRIES):
                    wait_drained(sp, st, (stage, what, 0, 0))
                    sp.dma_start(x_in[:, :, :], x_v[bass.ds(st.b + 3, 1)].rearrange("a p i d -> p (a i) d")
                                 ).then_inc(x_loaded, 16)
                if what == "maxima":
                    sp.wait_ge(m_turn, st.upto("S", 2, k + 1))
                    for g in range(G):
                        for part in range(2):
                            row = 3 * HD + part
                            sp.dma_start(
                                q_rows[row:row + 3 * KB + 1:KB, 1 - st.parity, 8 * k:8 * k + 8, g, :],
                                m_turned[KB * g:KB * g + KB, k, part, :]).then_inc(m_in_rows, 16)
                if (stage, what, k) == ("B", "down", LAST_CHUNK):
                    wait_drained(sp, st, (stage, what, 0, 0))
                    sp.dma_start(out_v[bass.ds(st.b - 1, 1)].rearrange("a p i d -> p (a i) d"), y[:, :, :]
                                 ).then_inc(y_free, 16)

            run(sp, piece)
            sp.wait_ge(y_free, 16 + 16 * ENTRIES)

        @block.tensor
        def _(pe):
            mm = nc.tensor.matmul
            pe.wait_ge(first_loaded, 16)
            pe.wait_ge(ffn_ready, 2)

            def begin(st, use, after=None):
                if after and st.slot(after) != st.slot(use):
                    wait_drained(pe, st, after)
                wait_for(pe, drained[st.slot(use)], st.work(use) - 1)
                return bank(st, use)

            def turn_tiles(st, use, src, after=None):
                ps = begin(st, use, after)
                for i in range(TILES):
                    last = nc.tensor.transpose(ps[:, P * i:P * i + P], src[:, P * i:P * i + P], ident)
                last.then_inc(filled[st.slot(use)], 1)

            def three_passes(ps, w_a, w_b, x_a, x_b, start):
                mm(ps, w_a, x_a, start=start, stop=False, skip_group_check=True)
                mm(ps, w_a, x_b, start=False, stop=False, skip_group_check=True)
                return mm(ps, w_b, x_a, start=False, stop=True, skip_group_check=True)

            def piece(st, stage, what, k):
                uses = work_uses((stage, what, k))
                if (what, k) == ("weights", 2):
                    pe.wait_ge(params_loaded, 16)
                    mm(mix[:, 0:D], par("ln_b"), par("wo"), start=True, stop=True).then_inc(bias_product, 1)
                elif what in ("keys", "queries", "values"):
                    x2 = ln["ln2"]
                    a = {"keys": WK, "queries": P * k, "values": WV}[what]
                    if what == "keys":
                        s = PLANS["FSPB"].slot[LN2_TURN]
                        if st.slot(uses[0]) != s:
                            pe.wait_ge(drained[s], st.work_before(s))
                    ps = begin(st, uses[0])
                    three_passes(ps, w_hi[:, a:a + P], w_lo[:, a:a + P], x2["hi"][:, :], x2["lo"][:, :], True
                                 ).then_inc(filled[st.slot(uses[0])], 1)
                elif what == "scores":
                    t, heads = SCORE_TILES[k]
                    n = KB * (t + 1)
                    if k == 0:
                        pe.wait_ge(q_done, st.upto("S", G, G))
                        pe.wait_ge(k_placed, st.upto("S", 1, 1))
                    ps = begin(st, uses[0])
                    h, nh = heads[0], len(heads)
                    mm(ps[:, 0:n * nh], q_rows[:, 1 - st.parity, t, :, :],
                       k_diag[:, 1 - st.parity, 0:t + 1, h:h + nh, :].rearrange("p u h k -> p u (h k)"),
                       start=True, stop=False, skip_group_check=True)
                    mm(ps[:, (n - KB) * nh:n * nh], mask_s[:, :], eye[:, :].unsqueeze(1).to_broadcast([P, nh, KB]),
                       start=False, stop=True, skip_group_check=True).then_inc(filled[st.slot(uses[0])], 1)
                elif what == "probs":
                    if k == 0:
                        pe.wait_ge(m_in_rows, st.upto("P", 2 * 2 * G * 16, 2 * 2 * G * 16))
                    for e in range(k, min(k + 2, len(UNITS))):
                        u, g, n = UNITS[e]
                        wait_for(pe, exp_done, st.upto("P", len(UNITS), e + 1 - ST_BANKS))
                        o = st_ps[:, e % ST_BANKS, 0:n * (TOKENS - KB * u)]
                        mm(o, k_diag[:, st.parity, u, :, :],
                           q_rows[:, st.parity, u:BLOCKS, g:g + n, :].rearrange("p t g q -> p t (g q)"),
                           start=True, stop=False, skip_group_check=True)
                        mm(o[:, 0:KB * n], mask_t[:, :], eye[:, :].unsqueeze(1).to_broadcast([P, n, KB]),
                           start=False, stop=True, skip_group_check=True).then_inc(st_filled, 1)
                elif what == "mix":
                    w = TOKENS - KB * k
                    pe.wait_ge(exp_done, st.upto("P", len(UNITS), UNITS_UPTO[k]))
                    if k == 0:
                        pe.wait_ge(v_done, st.upto("P", 1, 1))
                        wait_for(pe, num_out, st.upto("P", 1, 0))
                    for g in range(G):
                        last = mm(mix[KB * g:KB * g + KB, KB * k:TOKENS], v_diag[:, st.parity, k, :], probs[:, k % PROBS_RING, g, 0:w],
                                  start=(k == 0), stop=(k == BLOCKS - 1), skip_group_check=True)
                    last.then_inc(mix_done, 1)
                elif what == "sums":
                    use = (stage, what, 0, 0)
                    if k == 0:
                        pe.wait_ge(sum_done, st.upto("B", ADDED, ADDED))
                        begin(st, use)
                    ps = bank(st, use)
                    for u in [None] if k == 0 else range(ADDED, BLOCKS):
                        for g in range(G):
                            o, e = ((ps[KB * g:KB * g + KB, :], prob_sum[:, g, :]) if k == 0 else
                                    (ps[KB * g:KB * g + KB, KB * u:TOKENS], probs[:, u % PROBS_RING, g, 0:TOKENS - KB * u]))
                            last = mm(o, par("block"), e, start=(k == 0), stop=(u == BLOCKS - 1), skip_group_check=True)
                    if k == 1:
                        last.then_inc(filled[st.slot(use)], 1)
                elif what == "turn_out":
                    pe.wait_ge(num_out, st.upto("B", 1, 1))
                    turn_tiles(st, uses[0], num_t)
                    turn_tiles(st, uses[1], den_t, after=("B", "sums", 0, 0))
                elif what == "turn":
                    L = ln[k]
                    pe.wait_ge(L["s_xn"], st.upto(stage, 1, 1))
                    turn_tiles(st, uses[0], L["xn"][:, :, :].rearrange("p i d -> p (i d)"))
                elif what == "hidden":
                    L, F = ln["ln1" if stage == "F" else "ln3"], ffn[stage]
                    for j in range(2):
                        ps = begin(st, uses[j], (stage, "turn", "ln1" if stage == "F" else "ln3", 0) if k == j == 0 else None)
                        w = wgu_s[:, HIDDEN * j + P * k:HIDDEN * j + P * k + P]
                        mm(ps, w, L["hi"][:, :], start=True, stop=False)
                        mm(ps, w, L["lo"][:, :], start=False, stop=True).then_inc(filled[st.slot(uses[j])], 1)
                elif what == "down":
                    F = ffn[stage]
                    use, after = (stage, what, 0, 0), None
                    if k in UPS[stage]:
                        pe.wait_ge(F["s_h"], st.upto(stage, len(UPS[stage]), UPS[stage].index(k) + 1))
                    else:
                        after = (stage, "hidden", k, 1)
                    if k == 0:
                        begin(st, use, after)
                    elif after:
                        wait_drained(pe, st, after)
                    for i in range(TILES):
                        last = mm(bank(st, use)[:, P * i:P * i + P], F["h"][:, k, P * i:P * i + P], wd_s[:, P * k:P * k + P],
                                  start=(i == 0 and k == 0), stop=(k == LAST_CHUNK), skip_group_check=True)
                    if k == LAST_CHUNK:
                        last.then_inc(filled[st.slot(use)], 1)
                elif what == "out_proj":
                    L = ln["inner"]
                    ps = begin(st, uses[0], after=("B", "turn", "inner", 0))
                    for i in range(TILES):
                        o, t = ps[:, P * i:P * i + P], slice(P * i, P * i + P)
                        mm(o, L["hi"][:, t], wo_hi[:, :], start=(i == 0), stop=False, skip_group_check=True)
                        mm(o, L["hi"][:, t], wo_lo[:, :], start=False, stop=False, skip_group_check=True)
                        last = mm(o, L["lo"][:, t], wo_hi[:, :], start=False, stop=True, skip_group_check=True)
                    last.then_inc(filled[st.slot(uses[0])], 1)

            run(pe, piece)

        @block.scalar
        def _(act):
            activate = nc.scalar.activation

            def piece(st, stage, what, k):
                uses = work_uses((stage, what, k))
                if what in ("keys", "queries"):
                    if what == "keys":
                        i, scale, bias = 0, 1.0, par("bk")
                        wait_for(act, q_done, st.upto("S", G, 0))
                    else:
                        i, scale, bias = (k + 1) % 2, QSCALE, bq_s[:, k:k + 1]
                        if k == 1:
                            act.wait_ge(k_done, st.upto("S", 1, 1))
                        elif k > 1:
                            act.wait_ge(q_done, st.upto("S", G, k - 1))
                    wait_filled(act, st, uses[0])
                    activate(q_hi[:, i, :], bank(st, uses[0]), ACT.Identity, bias=bias, scale=scale).then_inc(q_high, 1)
                    activate(q_f[:, i, :], bank(st, uses[0]), ACT.Identity, bias=bias, scale=scale
                             ).then_inc(drained[st.slot(uses[0])], 1)
                elif what == "values":
                    wait_filled(act, st, uses[0])
                    activate(v_turned[:, :], bank(st, uses[0]), ACT.Identity, bias=par("bv")).then_inc(drained[st.slot(uses[0])], 1)
                elif what == "probs":
                    for e in range(k, min(k + 2, len(UNITS))):
                        u, g, n = UNITS[e]
                        if g == 0:
                            free_slot(st, u)
                        act.wait_ge(st_filled, st.upto("P", len(UNITS), e + 1))
                        activate(probs[:, u % PROBS_RING, g:g + n, 0:TOKENS - KB * u].rearrange("p g (t q) -> p g t q", q=KB),
                                 st_ps[:, e % ST_BANKS, 0:n * (TOKENS - KB * u)].rearrange("p (t g q) -> p g t q", g=n, q=KB),
                                 ACT.Exp).then_inc(exp_done, 1)
                elif what == "norm" and st.stages not in NORM_ON_VECTOR:
                    L = ln[k]
                    act.wait_ge(L["s_shift"], st.upto(stage, 1, 1))
                    for i in range(TILES):
                        last = activate(L["xn"][:, i, :], L["src"][:, i, :], ACT.Identity, bias=L["shift"][:, i:i + 1],
                                        scale=L["rstd"][:, i:i + 1])
                    last.then_inc(L["s_xn"], 1)
                elif what == "sums":
                    if k == 0:
                        act.wait_ge(mix_done, st.upto("B", BLOCKS, BLOCKS))
                        nc.scalar.copy(num_t[:, :], mix[:, :]).then_inc(num_out, 1)
                    else:
                        use = (stage, what, 0, 0)
                        wait_filled(act, st, use)
                        nc.scalar.copy(den_t[:, :], bank(st, use)).then_inc(drained[st.slot(use)], 1)
                elif what == "turn":
                    wait_filled(act, st, uses[0])
                    nc.scalar.copy(ln[k]["hi"][:, :], bank(st, uses[0])).then_inc(ln[k]["s_hi"], 1)
                elif what == "hidden":
                    F = ffn[stage]
                    wait_filled(act, st, uses[0])
                    activate(F["th"][:, k % 2, :], bank(st, uses[0]), ACT.Tanh, scale=TANH_SCALE).then_inc(F["s_th"], 1)
                    if (stage, k) in UP_ON_GPSIMD:
                        wait_filled(act, st, uses[1])
                        nc.scalar.copy(F["up"][:, k, :], bank(st, uses[1])).then_inc(drained[st.slot(uses[1])], 1)

            def free_slot(st, u):
                old = u - PROBS_RING
                wait_for(act, mix_done, st.upto("P", BLOCKS, old + 1))
                if old >= 0:
                    act.wait_ge(sum_done, st.upto("P", ADDED, min(max(old + 1, 2), ADDED)))
                elif u == 0:
                    wait_for(act, sum_done, st.upto("P", ADDED, 0))
                if old + BLOCKS == ADDED and "B" in st.stages:
                    wait_filled(act, st, ("B", "sums", 0, 0))

            run(act, piece)

        @block.vector
        def _(dve):
            v = nc.vector
            dve.wait_ge(ints_loaded, 32)
            v.tensor_scalar(wgu_s[:, :], wgu_i[:, :], WSCALE, None, ALU.mult).then_inc(ffn_ready, 1)
            v.tensor_scalar(wd_s[:, :], wd_i[:, :], WSCALE, None, ALU.mult).then_inc(ffn_ready, 1)

            def weights(k):
                if k == 0:
                    dve.wait_ge(params_loaded, 16)
                    v.tensor_copy(w_hi[:, :], par("wqkv")).then_inc(w_high, 1)
                    v.tensor_scalar(wo_g[:, :], par("wo"), par("ln_g"), None, ALU.mult).then_inc(wo_scaled, 1)
                    v.tensor_copy(mask_s[:, :], par("mask_s")).then_inc(weights_ready, 1)
                    v.tensor_copy(mask_t[:, :], par("mask_t")).then_inc(weights_ready, 1)
                    v.tensor_copy(eye[:, :], par("eye")).then_inc(weights_ready, 1)
                    v.tensor_scalar(bq_s[:, :], par("bq"), QSCALE, None, ALU.mult).then_inc(weights_ready, 1)
                elif k == 1:
                    dve.wait_ge(w_high, 1)
                    v.tensor_tensor(w_lo[:, :], par("wqkv"), w_hi[:, :], ALU.subtract).then_inc(weights_ready, 1)
                else:
                    dve.wait_ge(wo_scaled, 1)
                    v.tensor_copy(wo_hi[:, :], wo_g[:, :]).then_inc(w_high, 1)
                    dve.wait_ge(w_high, 2)
                    v.tensor_tensor(wo_lo[:, :], wo_g[:, :], wo_hi[:, :], ALU.subtract).then_inc(weights_ready, 1)
                    dve.wait_ge(bias_product, 1)
                    v.tensor_tensor(bo_all[:, :], mix[:, 0:D], par("bo"), ALU.add).then_inc(weights_ready, 1)

            def piece(st, stage, what, k):
                uses = work_uses((stage, what, k))
                if what == "add" and st.stages in ADD_ON_VECTOR:
                    add(v, st, k)
                if what == "weights":
                    weights(k)
                if what in ("keys", "queries"):
                    wait_drained(dve, st, uses[0])
                    i = 0 if what == "keys" else (k + 1) % 2
                    o, low, s = ((k_rows[:, :].rearrange("p (u c) -> p u c", c=KB), par("low_k"), k_done)
                                 if what == "keys" else (q_rows[:, 1 - st.parity, :, k, :], par("low_q"), q_done))
                    v.scalar_tensor_tensor(out=o, in0=q_hi[:, i, :].rearrange("p (u c) -> p u c", c=KB), scalar=low,
                                           in1=q_f[:, i, :].rearrange("p (u c) -> p u c", c=KB),
                                           op0=ALU.mult, op1=ALU.add).then_inc(s, 1)
                if what == "keys":
                    dve.wait_ge(k_done, st.upto("S", 1, 1))
                    for h in range(H):
                        r = slice(KB * h, KB * h + KB)
                        last = v.tensor_copy(k_diag[r, 1 - st.parity, :, h, :], k_rows[r, :].rearrange("p (u c) -> p u c", c=KB))
                    last.then_inc(k_placed, 1)
                elif what == "values":
                    wait_drained(dve, st, uses[0])
                    v.transpose(v_diag[:, 1 - st.parity, :, :].rearrange("p u c -> p (u c)"), v_turned[:, :]).then_inc(v_done, 1)
                elif what == "scores":
                    t, heads = SCORE_TILES[k]
                    n, nh = KB * (t + 1), len(heads)
                    wait_filled(dve, st, uses[0])
                    v.tensor_reduce(m_all[:, t // 8, heads[0]:heads[0] + nh, t % 8],
                                    bank(st, uses[0])[:, 0:n * nh].rearrange("p (u h k) -> p h u k", h=nh, k=KB), AX.XY, ALU.max
                                    ).then_inc(drained[st.slot(uses[0])], 1)
                elif what == "maxima":
                    last_tile = (FIRST_HALF if k == 0 else len(SCORE_TILES)) - 1
                    wait_drained(dve, st, ("S", "scores", last_tile, 0))
                    m = m_all[:, k, :, :].rearrange("p h t -> p (h t)")
                    v.tensor_copy(m_parts[:, k, 0, :], m).then_inc(m_high, 1)
                    dve.wait_ge(m_high, st.upto("S", 2, k + 1))
                    v.tensor_tensor(m_parts[:, k, 1, :], m, m_parts[:, k, 0, :], ALU.subtract).then_inc(m_split, 1)
                    dve.wait_ge(m_split, st.upto("S", 2, k + 1))
                    wait_for(dve, m_in_rows, st.upto("S", 4 * G * 16, 0))
                    v.transpose(m_turned[:, k, :, :].rearrange("p a c -> p (a c)"),
                                m_parts[:, k, :, :].rearrange("p a c -> p (a c)")).then_inc(m_turn, 1)
                elif what == "turn_out":
                    wait_filled(dve, st, uses[1])
                    v.reciprocal(rden[:, :], bank(st, uses[1]).rearrange("p (c d) -> p c d", d=HD)[:, :, 0]
                                 ).then_inc(drained[st.slot(uses[1])], 1)
                    wait_drained(dve, st, uses[1])
                    v.tensor_tensor(attended[:, :, :].rearrange("p i (c d) -> p (i c) d", d=HD),
                                    bank(st, uses[0]).rearrange("p (c d) -> p c d", d=HD),
                                    rden[:, :].unsqueeze(2).to_broadcast([P, TILES * G * H, HD]), ALU.mult
                                    ).then_inc(drained[st.slot(uses[0])], 1)
                elif what == "stats":
                    L = ln[k]
                    if k == "ln1":
                        dve.wait_ge(x_loaded, st.upto("F", 16, 16))
                    else:
                        wait_drained(dve, st, {"ln2": ("F", "down", 0, 0), "inner": ("B", "turn_out", 0, 0),
                                               "ln3": ("B", "out_proj", 0, 0)}[k])
                    for i in range(TILES):
                        v.bn_stats(L["bn"][:, i, :], L["src"][:, i, :]).then_inc(L["s_bn"], 1)
                    dve.wait_ge(L["s_bn"], st.upto(stage, TILES, TILES))
                    v.memset(waits_here[:, :], 0.0)
                    for i in range(TILES):
                        v.bn_aggr(L["mv"][:, i, :], L["bn"][:, i, :]).then_inc(L["s_mv"], 1)
                elif what == "norm" and st.stages in NORM_ON_VECTOR:
                    L = ln[k]
                    dve.wait_ge(L["s_rstd"], st.upto(stage, 1, 1))
                    for i in range(TILES):
                        last = v.tensor_scalar(L["xn"][:, i, :], L["src"][:, i, :], L["mv"][:, i, 0:1], L["rstd"][:, i:i + 1],
                                               ALU.subtract, ALU.mult)
                    last.then_inc(L["s_xn"], 1)
                elif what == "turn":
                    L = ln[k]
                    dve.wait_ge(L["s_hi"], st.upto(stage, 1, 1))
                    v.tensor_tensor(L["lo"][:, :], bank(st, uses[0]), L["hi"][:, :], ALU.subtract
                                    ).then_inc(drained[st.slot(uses[0])], 1)
                elif what == "gated":
                    uses = work_uses((stage, "hidden", k))
                    F = ffn[stage]
                    dve.wait_ge(F["s_th"], st.upto(stage, CHUNKS, k + 1))
                    v.scalar_tensor_tensor(out=F["h"][:, k, :], in0=F["th"][:, k % 2, :], scalar=1.0, in1=bank(st, uses[0]),
                                           op0=ALU.add, op1=ALU.mult).then_inc(drained[st.slot(uses[0])], 1)
                    if (stage, k) not in UP_ON_GPSIMD:
                        wait_filled(dve, st, uses[1])
                        wait_drained(dve, st, uses[0])
                        v.tensor_tensor(F["h"][:, k, :], F["h"][:, k, :], bank(st, uses[1]), ALU.mult
                                        ).then_inc(drained[st.slot(uses[1])], 1)
                elif what == "down" and k == LAST_CHUNK:
                    uses = [(stage, what, 0, 0)]
                    wait_filled(dve, st, uses[0])
                    if stage == "B":
                        dve.wait_ge(y_free, 16 + st.upto("B", 16, 0))
                    else:
                        wait_for(dve, x_mid_done, st.upto("F", 1, 0))
                    o, res = (x_front, x_in) if stage == "F" else (y, x_att)
                    v.scalar_tensor_tensor(out=flat(o), in0=bank(st, uses[0]), scalar=FFN_SCALE, in1=flat(res),
                                           op0=ALU.mult, op1=ALU.add).then_inc(drained[st.slot(uses[0])], 1)
                elif what == "out_proj":
                    wait_filled(dve, st, uses[0])
                    dve.wait_ge(x_mid_done, st.upto("B", 1, 1))
                    v.tensor_tensor(x_att[:, :, :], bank(st, uses[0]).rearrange("p (i d) -> p i d", d=D), entry(x_mid, st.b - 1),
                                    ALU.add).then_inc(drained[st.slot(uses[0])], 1)

            def flat(t):
                return t[:, :, :].rearrange("p i d -> p (i d)")

            run(dve, piece)

        @block.gpsimd
        def _(pool):
            g_ = nc.gpsimd
            g_.memset(k_diag[:, :, :, :, :], 0.0).then_inc(k_cleared, 1)
            g_.memset(y[:, 0, 0:1], 0.0).then_inc(y_free, 16)
            pool.wait_ge(first_loaded, 16)

            def piece(st, stage, what, k):
                uses = work_uses((stage, what, k))
                if what == "add" and st.stages not in ADD_ON_VECTOR:
                    add(g_, st, k)
                elif what == "stats":
                    L = ln[k]
                    pool.wait_ge(L["s_mv"], st.upto(stage, TILES, TILES))
                    g_.tensor_tensor(L["var"][:, :], L["mv"][:, :, 1], par("eps"), ALU.add).then_inc(L["s_var"], 1)
                    pool.wait_ge(L["s_var"], st.upto(stage, 1, 1))
                    g_.tensor_tensor(L["rstd"][:, :], L["var"][:, :], par("neg_half"), ALU.pow).then_inc(L["s_rstd"], 1)
                    pool.wait_ge(L["s_rstd"], st.upto(stage, 1, 1))
                    g_.tensor_tensor(L["minus"][:, :], L["rstd"][:, :], par("minus_one"), ALU.mult).then_inc(L["s_minus"], 1)
                    pool.wait_ge(L["s_minus"], st.upto(stage, 1, 1))
                    g_.tensor_tensor(L["shift"][:, :], L["mv"][:, :, 0], L["minus"][:, :], ALU.mult).then_inc(L["s_shift"], 1)
                elif what == "gated" and (stage, k) in UP_ON_GPSIMD:
                    F = ffn[stage]
                    for j in range(2):
                        wait_drained(pool, st, (stage, "hidden", k, j))
                    g_.tensor_tensor(F["h"][:, k, :], F["h"][:, k, :], F["up"][:, k, :], ALU.mult
                                     ).then_inc(F["s_h"], 1)
                elif what == "carry":
                    wait_drained(pool, st, ("F", "down", 0, 0))
                    if st.stages == "F":
                        pool.wait_ge(weights_ready, SETUP)
                    g_.tensor_tensor(entry(x_mid, st.b + 2), x_front[:, :, :],
                                     bo_all[:, :].unsqueeze(1).to_broadcast([P, TILES, D]), ALU.add).then_inc(x_mid_done, 1)

            run(pool, piece)

    return nc


def layout(inputs):
    f = {n[len("L0_attn_"):]: np.asarray(a) for n, a in inputs.items() if n.startswith("L0_attn_")}
    one = np.float32

    def rows(w, keep):
        o = np.zeros(w.shape[:-2] + (H, 4, HD), one)
        for slot in range(3):
            o[..., slot, :] = w
        return o.reshape(keep + (-1,))

    wq, wk = rows(f["Wq"].reshape(D, G, H, HD), (D,)), rows(f["Wk"].reshape(D, H, HD), (D,))
    bq = rows(f["bq"].reshape(G, H, HD), (G,)).T
    wv, bv = np.zeros((D, H, H, HD), one), np.zeros((H, H, HD), one)
    for h in range(H):
        wv[:, h, h], bv[h, h] = f["Wv"][:, HD * h:HD * h + HD], f["bv"][HD * h:HD * h + HD]
    bk = rows(f["bk"].reshape(H, HD), ())
    bk = bk.reshape(H, 4, HD)
    bk[:, 3, 0:2] = -1.0
    row = np.arange(P)
    slot = (row // HD) % 4
    a, k = np.arange(P)[:, None], np.arange(P)[None, :] % KB
    cols = {
        "wqkv": np.concatenate([wq, wk, wv.reshape(D, P)], 1), "wo": f["Wo"], "ln_b": np.repeat(f["ln_b"][:, None], P, 1),
        "bo": np.repeat(f["bo"][None], P, 0), "bv": bv.reshape(P, 1), "bq": bq, "bk": bk.reshape(P, 1),
        "ln_g": f["ln_g"][:, None], "ident": np.eye(P, dtype=one),
        "mask_s": np.where((a < KB) & (a > k), one(MASKED), one(0)),
        "mask_t": np.where((a < KB) & (a < k), one(MASKED), one(0)),
        "eye": np.eye(P, KB, dtype=one), "block": (row[:, None] // KB == np.arange(H * HD)[None] // HD).astype(one),
        "low_q": np.where(slot == 2, one(-1), one(0))[:, None], "low_k": np.where(slot == 1, one(-1), one(0))[:, None],
        "neg_half": np.full((P, TILES), -0.5, one), "eps": np.full((P, TILES), EPS, one),
        "minus_one": np.full((P, TILES), -1, one), "zero": np.zeros((P, 1), one),
    }
    packed = np.empty((P, PACKED), one)
    for name, (lo, hi) in PACK.items():
        packed[:, lo:hi] = cols[name]
    wg, wu, wd = (np.asarray(inputs["L0_ffn_" + n]) for n in ("w_gate", "w_up", "w_down"))
    wgu = np.ascontiguousarray(np.concatenate([wg, wu], 0).T)
    wd = np.ascontiguousarray(wd.T.reshape(CHUNKS, P, D).transpose(1, 0, 2).reshape(P, HIDDEN))
    return np.ascontiguousarray(f["x"]), packed, wgu, wd


def kernel(**inputs):
    import concourse.bacc as bacc
    from concourse.bass_utils import run_bass_kernel_spmd

    nc = bacc.Bacc("TRN2", target_bir_lowering=False, num_devices=1)
    arrays, args = {}, []
    for name, a in zip(("x", "packed", "wgu", "wd"), layout(inputs)):
        arrays[name] = a
        args.append(nc.dram_tensor(name, a.shape, mybir.dt.from_np(a.dtype), kind="ExternalInput").ap())
    out = nc.dram_tensor("out", (ENTRIES, TOKENS, D), F32, kind="ExternalOutput").ap()
    macaron(nc, *args, out)
    r = run_bass_kernel_spmd(nc, [arrays], core_ids=[0])
    return r.results[0]["out"]
```
